# Optimizing a Trainium2 kernel written in Bass

```python
import numpy as np
import jax
import jax.numpy as jnp

def _softmax(x, axis=-1):
    return jax.nn.softmax(x, axis=axis)

def _gelu(x):
    return jax.nn.gelu(x, approximate=True)

def _silu(x):
    return jax.nn.silu(x)

def _sigmoid(x):
    return jax.nn.sigmoid(x)

def _layernorm(x, axis=-1, eps=1e-05):
    m = jnp.mean(x, axis=axis, keepdims=True)
    v = jnp.var(x, axis=axis, keepdims=True)
    return (x - m) / jnp.sqrt(v + eps)

def _scatter_add(tgt, idx, src, axis=0):
    return tgt.at[idx].add(src)

def _segment_sum(src, seg, n):
    return jax.ops.segment_sum(src, seg, n)
kernel_name = 'mk_decoder_postln_d2_seqx_r4_15ddf2'

def setup_inputs(seed: int=0):
    np.random.seed(seed)
    _w = jnp.asarray

    def _rec_inputs():
        import jax
        import jax.numpy as jnp
        _rk = jax.random.key(seed)
        x = 7.22e-05 + 1 * jax.random.normal(jax.random.fold_in(_rk, 1), (2, 512, 256), jnp.float32)
        _lenS = 512 - jax.random.randint(jax.random.fold_in(_rk, 7), (2,), 0, max(1, 512 // 4) + 1, jnp.int32)
        _lenS2 = 1024 - jax.random.randint(jax.random.fold_in(_rk, 8), (2,), 0, max(1, 1024 // 4) + 1, jnp.int32)
        _ctx_768P = jax.random.normal(jax.random.fold_in(_rk, 11), (2, 16, 192), jnp.float32)
        _ctx_768c = jax.random.dirichlet(jax.random.fold_in(_rk, 511), 0.3 * jnp.ones((16,), jnp.float32), (2, 1024))
        _ctx_768t = jnp.einsum('bsk,bkd->bsd', _ctx_768c, _ctx_768P)
        _ctx_768t = _ctx_768t * jax.lax.rsqrt(jnp.mean(jnp.square(_ctx_768t)) + 1e-12) * 0.953939
        ctx_768 = -0.000191848 + 0.999787 * (_ctx_768t + 0.3 * jax.random.normal(jax.random.fold_in(_rk, 611), (2, 1024, 192), jnp.float32))
        return (x, ctx_768)
    x, ctx_768 = _rec_inputs()

    def _L0_attn_setup():
        import jax, jax.numpy as jnp
        import numpy as np
        B, T, C, H = (2, 512, 256, 16)
        key = jax.random.key(seed)
        ks = jax.random.split(key, 6)
        x = jax.random.normal(ks[0], (B, T, C), dtype=jnp.float32)
        wq = jax.random.normal(ks[1], (C, H * 3), dtype=jnp.float32) * C ** (-0.5)
        wk = jax.random.normal(ks[2], (C, H * 3), dtype=jnp.float32) * C ** (-0.5)
        wv = jax.random.normal(ks[3], (C, C), dtype=jnp.float32) * C ** (-0.5)
        wo = jax.random.normal(ks[4], (C, C), dtype=jnp.float32) * C ** (-0.5)
        dirs = jax.random.normal(ks[5], (H, 3), dtype=jnp.float32)
        head_dirs = dirs / jnp.linalg.norm(dirs, axis=1, keepdims=True)
        scale = jnp.full((1,), 1.0 / np.sqrt(3.0), dtype=jnp.float32)
        return {'x': x, 'wq': wq, 'wk': wk, 'wv': wv, 'wo': wo, 'head_dirs': head_dirs, 'scale': scale}
    _L0_attn_all = _L0_attn_setup()
    _L0_attn_in = {k: v for k, v in _L0_attn_all.items() if k in ('wq', 'wk', 'wv', 'wo', 'head_dirs', 'scale')}
    del _L0_attn_all

    def _L0_xattn_setup():
        import jax, jax.numpy as jnp
        import numpy as np
        NUM_HEADS = 16
        CLAMP = 10000.0
        key = jax.random.key(seed)
        ks = jax.random.split(key, 8)
        B, Nq, Nkv, Cq, Ckv = (4, 512, 512, 256, 192)
        s_q = 1.0 / np.sqrt(Cq)
        s_kv = 1.0 / np.sqrt(Ckv)
        return {'query': jax.random.normal(ks[0], (B, Nq, Cq), jnp.float32), 'key_value': jax.random.normal(ks[1], (B, Nkv, Ckv), jnp.float32), 'Wq': jax.random.normal(ks[2], (Cq, Cq), jnp.float32) * s_q, 'bq': jnp.zeros((Cq,), jnp.float32), 'Wk': jax.random.normal(ks[3], (Ckv, Cq), jnp.float32) * s_kv, 'bk': jnp.zeros((Cq,), jnp.float32), 'Wv': jax.random.normal(ks[4], (Ckv, Cq), jnp.float32) * s_kv, 'bv': jnp.zeros((Cq,), jnp.float32), 'Wo': jax.random.normal(ks[5], (Cq, Cq), jnp.float32) * s_q, 'bo': jnp.zeros((Cq,), jnp.float32)}
    _L0_xattn_all = _L0_xattn_setup()
    _L0_xattn_in = {k: v for k, v in _L0_xattn_all.items() if k in ('Wq', 'bq', 'Wk', 'bk', 'Wv', 'bv', 'Wo', 'bo')}
    del _L0_xattn_all

    def _L0_ffn_setup():
        import jax, jax.numpy as jnp
        import numpy as np
        import math
        D_IN = 256
        FEATURES = (1024, 1024, 256)
        BATCH, SEQ = (8, 512)

        def _conn_dense(kernel_bool, x):
            w = jnp.where(kernel_bool, jnp.float32(1.0), jnp.float32(-1.0))
            return x @ w
        key = jax.random.key(seed)
        kx, kk0, kk1, kk2 = jax.random.split(key, 4)
        x = jax.random.normal(kx, (BATCH, SEQ, D_IN), dtype=jnp.float32)
        k0 = jax.random.randint(kk0, (2 * D_IN, FEATURES[0]), 0, 2).astype(jnp.bool_)
        k1 = jax.random.randint(kk1, (FEATURES[0], FEATURES[1]), 0, 2).astype(jnp.bool_)
        k2 = jax.random.randint(kk2, (FEATURES[1], FEATURES[2]), 0, 2).astype(jnp.bool_)
        s0 = jnp.asarray(1.0 / math.sqrt(2 * D_IN), dtype=jnp.float32)
        s1 = jnp.asarray(1.0 / math.sqrt(FEATURES[0]), dtype=jnp.float32)
        s2 = jnp.asarray(1.0 / math.sqrt(FEATURES[1]), dtype=jnp.float32)
        return {'x': x, 'k0': k0, 'k1': k1, 'k2': k2, 's0': s0, 's1': s1, 's2': s2}
    _L0_ffn_all = _L0_ffn_setup()
    _L0_ffn_in = {k: v for k, v in _L0_ffn_all.items() if k in ('k0', 'k1', 'k2', 's0', 's1', 's2')}
    del _L0_ffn_all

    def _L1_attn_setup():
        import jax, jax.numpy as jnp
        import numpy as np
        import math
        INPUT_WIDTH = 256
        KEY_WIDTH = 64
        VALUE_WIDTH = 64
        NUM_HEADS = 16
        NUM_GROUPS = 4
        HEADS_PER_GROUP = NUM_HEADS // NUM_GROUPS
        key = jax.random.key(seed)
        k_x, k_q, k_k, k_v, k_p = jax.random.split(key, 5)
        n, s = (2, 512)

        def lin(k, fan_in, fan_out):
            bound = 1.0 / math.sqrt(fan_in)
            return jax.random.uniform(k, (fan_in, fan_out), minval=-bound, maxval=bound, dtype=jnp.float32)
        return {'X': jax.random.normal(k_x, (n, s, INPUT_WIDTH), dtype=jnp.float32), 'Wq': lin(k_q, INPUT_WIDTH, NUM_HEADS * KEY_WIDTH), 'Wk': lin(k_k, INPUT_WIDTH, NUM_GROUPS * KEY_WIDTH), 'Wv': lin(k_v, INPUT_WIDTH, NUM_GROUPS * VALUE_WIDTH), 'Wpost': lin(k_p, NUM_HEADS * VALUE_WIDTH, INPUT_WIDTH)}
    _L1_attn_all = _L1_attn_setup()
    _L1_attn_in = {k: v for k, v in _L1_attn_all.items() if k in ('Wq', 'Wk', 'Wv', 'Wpost')}
    del _L1_attn_all

    def _L1_xattn_setup():
        import jax, jax.numpy as jnp
        import numpy as np
        HEADS = 8
        DIM_HEAD = 64
        SCALE = DIM_HEAD ** (-0.5)
        key = jax.random.key(seed)
        ks = jax.random.split(key, 7)
        b, n, m = (4, 512, 256)
        qd, cd, inner = (256, 192, HEADS * DIM_HEAD)
        s = lambda fan_in: 1.0 / np.sqrt(fan_in)
        return {'x': jax.random.normal(ks[0], (b, n, qd), jnp.float32), 'context': jax.random.normal(ks[1], (b, m, cd), jnp.float32), 'Wq': jax.random.normal(ks[2], (qd, inner), jnp.float32) * s(qd), 'Wk': jax.random.normal(ks[3], (cd, inner), jnp.float32) * s(cd), 'Wv': jax.random.normal(ks[4], (cd, inner), jnp.float32) * s(cd), 'Wout': jax.random.normal(ks[5], (inner, qd), jnp.float32) * s(inner), 'bout': jax.random.normal(ks[6], (qd,), jnp.float32) * 0.01}
    _L1_xattn_all = _L1_xattn_setup()
    _L1_xattn_in = {k: v for k, v in _L1_xattn_all.items() if k in ('Wq', 'Wk', 'Wv', 'Wout', 'bout')}
    del _L1_xattn_all

    def _L1_ffn_setup():
        import jax, jax.numpy as jnp
        import numpy as np
        E = 8
        K = 2
        key = jax.random.key(seed)
        ks = jax.random.split(key, 8)
        B, T, d = (4, 512, 256)
        h = 4 * d // E
        s = 0.02
        X = jax.random.normal(ks[0], (B, T, d), jnp.float32)
        routing_W = jax.random.normal(ks[1], (E, d), jnp.float32) * s
        expert_bias = jnp.zeros((E,), jnp.float32)
        sW1 = jax.random.normal(ks[2], (d, h), jnp.float32) * s
        sb1 = jnp.zeros((h,), jnp.float32)
        sW2 = jax.random.normal(ks[3], (h, d), jnp.float32) * s
        sb2 = jnp.zeros((d,), jnp.float32)
        rW1 = jax.random.normal(ks[4], (E, d, h), jnp.float32) * s
        rb1 = jnp.zeros((E, h), jnp.float32)
        rW2 = jax.random.normal(ks[5], (E, h, d), jnp.float32) * s
        rb2 = jnp.zeros((E, d), jnp.float32)
        return dict(X=X, routing_W=routing_W, expert_bias=expert_bias, sW1=sW1, sb1=sb1, sW2=sW2, sb2=sb2, rW1=rW1, rb1=rb1, rW2=rW2, rb2=rb2)
    _L1_ffn_all = _L1_ffn_setup()
    _L1_ffn_in = {k: v for k, v in _L1_ffn_all.items() if k in ('routing_W', 'expert_bias', 'sW1', 'sb1', 'sW2', 'sb2', 'rW1', 'rb1', 'rW2', 'rb2')}
    del _L1_ffn_all
    return {'x': x, 'ctx_768': ctx_768, 'L0_attn_wq': _L0_attn_in['wq'], 'L0_attn_wk': _L0_attn_in['wk'], 'L0_attn_wv': _L0_attn_in['wv'], 'L0_attn_wo': _L0_attn_in['wo'], 'L0_attn_head_dirs': _L0_attn_in['head_dirs'], 'L0_attn_scale': _L0_attn_in['scale'], 'L0_xattn_Wq': _L0_xattn_in['Wq'], 'L0_xattn_bq': _L0_xattn_in['bq'], 'L0_xattn_Wk': _L0_xattn_in['Wk'], 'L0_xattn_bk': _L0_xattn_in['bk'], 'L0_xattn_Wv': _L0_xattn_in['Wv'], 'L0_xattn_bv': _L0_xattn_in['bv'], 'L0_xattn_Wo': _L0_xattn_in['Wo'], 'L0_xattn_bo': _L0_xattn_in['bo'], 'L0_ffn_k0': _L0_ffn_in['k0'], 'L0_ffn_k1': _L0_ffn_in['k1'], 'L0_ffn_k2': _L0_ffn_in['k2'], 'L0_ffn_s0': _L0_ffn_in['s0'], 'L0_ffn_s1': _L0_ffn_in['s1'], 'L0_ffn_s2': _L0_ffn_in['s2'], 'L1_attn_Wq': _L1_attn_in['Wq'], 'L1_attn_Wk': _L1_attn_in['Wk'], 'L1_attn_Wv': _L1_attn_in['Wv'], 'L1_attn_Wpost': _L1_attn_in['Wpost'], 'L1_xattn_Wq': _L1_xattn_in['Wq'], 'L1_xattn_Wk': _L1_xattn_in['Wk'], 'L1_xattn_Wv': _L1_xattn_in['Wv'], 'L1_xattn_Wout': _L1_xattn_in['Wout'], 'L1_xattn_bout': _L1_xattn_in['bout'], 'L1_ffn_routing_W': _L1_ffn_in['routing_W'], 'L1_ffn_expert_bias': _L1_ffn_in['expert_bias'], 'L1_ffn_sW1': _L1_ffn_in['sW1'], 'L1_ffn_sb1': _L1_ffn_in['sb1'], 'L1_ffn_sW2': _L1_ffn_in['sW2'], 'L1_ffn_sb2': _L1_ffn_in['sb2'], 'L1_ffn_rW1': _L1_ffn_in['rW1'], 'L1_ffn_rb1': _L1_ffn_in['rb1'], 'L1_ffn_rW2': _L1_ffn_in['rW2'], 'L1_ffn_rb2': _L1_ffn_in['rb2']}

def reference(x, ctx_768, L0_attn_wq, L0_attn_wk, L0_attn_wv, L0_attn_wo, L0_attn_head_dirs, L0_attn_scale, L0_xattn_Wq, L0_xattn_bq, L0_xattn_Wk, L0_xattn_bk, L0_xattn_Wv, L0_xattn_bv, L0_xattn_Wo, L0_xattn_bo, L0_ffn_k0, L0_ffn_k1, L0_ffn_k2, L0_ffn_s0, L0_ffn_s1, L0_ffn_s2, L1_attn_Wq, L1_attn_Wk, L1_attn_Wv, L1_attn_Wpost, L1_xattn_Wq, L1_xattn_Wk, L1_xattn_Wv, L1_xattn_Wout, L1_xattn_bout, L1_ffn_routing_W, L1_ffn_expert_bias, L1_ffn_sW1, L1_ffn_sb1, L1_ffn_sW2, L1_ffn_sb2, L1_ffn_rW1, L1_ffn_rb1, L1_ffn_rW2, L1_ffn_rb2):
    import jax
    import jax.numpy as jnp

    def _L0_attn_ref(x, wq, wk, wv, wo, head_dirs, scale):
        import jax, jax.numpy as jnp
        import numpy as np
        B, T, C, H = (2, 512, 256, 16)
        b, t, c = x.shape
        h = head_dirs.shape[0]
        hd = c // h
        q3 = (x @ wq).reshape(b, t, h, 3).transpose(0, 2, 1, 3)
        k3 = (x @ wk).reshape(b, t, h, 3).transpose(0, 2, 1, 3)
        v = (x @ wv).reshape(b, t, h, hd).transpose(0, 2, 1, 3)
        q_on_dir = jnp.einsum('bhtd,hd->bht', q3, head_dirs)
        k_on_dir = jnp.einsum('bhtd,hd->bht', k3, head_dirs)
        dot_scores = jnp.einsum('bhtd,bhsd->bhts', q3, k3) * scale
        geo_bias = q_on_dir[..., :, None] * k_on_dir[..., None, :]
        scores = dot_scores + geo_bias
        causal = jnp.tril(jnp.ones((t, t), dtype=bool))
        scores = jnp.where(causal, scores, -jnp.inf)
        attn = jax.nn.softmax(scores, axis=-1)
        out = jnp.einsum('bhts,bhsd->bhtd', attn, v)
        out = out.transpose(0, 2, 1, 3).reshape(b, t, c)
        return out @ wo

    def _L0_xattn_ref(query, key_value, Wq, bq, Wk, bk, Wv, bv, Wo, bo):
        import jax, jax.numpy as jnp
        import numpy as np
        NUM_HEADS = 16
        CLAMP = 10000.0
        B, Nq, Cq = query.shape
        Nkv = key_value.shape[1]
        H = NUM_HEADS
        D = Cq // H
        scale = D ** (-0.5)
        q = (query @ Wq + bq).reshape(B, Nq, H, D).transpose(0, 2, 1, 3)
        k = (key_value @ Wk + bk).reshape(B, Nkv, H, D).transpose(0, 2, 1, 3)
        v = (key_value @ Wv + bv).reshape(B, Nkv, H, D).transpose(0, 2, 1, 3)
        attn = jnp.einsum('bhqd,bhkd->bhqk', q, k) * scale
        attn = jnp.clip(attn, -CLAMP, CLAMP)
        attn = jax.nn.softmax(attn, axis=-1)
        attn = jnp.where(jnp.any(jnp.isnan(attn)), jnp.asarray(1.0 / Nkv, attn.dtype), attn)
        x = jnp.einsum('bhqk,bhkd->bqhd', attn, v).reshape(B, Nq, Cq)
        return x @ Wo + bo

    def _L0_ffn_ref(x, k0, k1, k2, s0, s1, s2):
        import jax, jax.numpy as jnp
        import numpy as np
        import math
        D_IN = 256
        FEATURES = (1024, 1024, 256)
        BATCH, SEQ = (8, 512)

        def _conn_dense(kernel_bool, x):
            w = jnp.where(kernel_bool, jnp.float32(1.0), jnp.float32(-1.0))
            return x @ w
        h = jnp.concatenate([x, -x], axis=-1)
        h = s0 * _conn_dense(k0, h)
        h = jax.nn.relu(h) * 2
        h = s1 * _conn_dense(k1, h)
        h = jax.nn.relu(h) * 2
        h = s2 * _conn_dense(k2, h)
        return h

    def _L1_attn_ref(X, Wq, Wk, Wv, Wpost):
        import jax, jax.numpy as jnp
        import numpy as np
        import math
        INPUT_WIDTH = 256
        KEY_WIDTH = 64
        VALUE_WIDTH = 64
        NUM_HEADS = 16
        NUM_GROUPS = 4
        HEADS_PER_GROUP = NUM_HEADS // NUM_GROUPS
        n, s, _ = X.shape
        Q = (X @ Wq).reshape(n, s, NUM_GROUPS, HEADS_PER_GROUP, KEY_WIDTH)
        K = (X @ Wk).reshape(n, s, NUM_GROUPS, KEY_WIDTH)
        V = (X @ Wv).reshape(n, s, NUM_GROUPS, VALUE_WIDTH)
        scale = 1.0 / math.sqrt(KEY_WIDTH)
        raw = jnp.einsum('bsgwe,btge->bstgw', Q, K * scale)
        attn = jax.nn.softmax(raw, axis=2)
        A = jnp.einsum('bstgw,btge->bsgwe', attn, V).reshape(n, s, NUM_HEADS * VALUE_WIDTH)
        P = A @ Wpost
        return X + P

    def _L1_xattn_ref(x, context, Wq, Wk, Wv, Wout, bout):
        import jax, jax.numpy as jnp
        import numpy as np
        HEADS = 8
        DIM_HEAD = 64
        SCALE = DIM_HEAD ** (-0.5)
        b, n, _ = x.shape
        m = context.shape[1]
        q = (x @ Wq).reshape(b, n, HEADS, DIM_HEAD)
        k = (context @ Wk).reshape(b, m, HEADS, DIM_HEAD)
        v = (context @ Wv).reshape(b, m, HEADS, DIM_HEAD)
        sim = jnp.einsum('bihd,bjhd->bhij', q, k) * SCALE
        attn = jax.nn.softmax(sim, axis=-1)
        out = jnp.einsum('bhij,bjhd->bihd', attn, v).reshape(b, n, HEADS * DIM_HEAD)
        return out @ Wout + bout

    def _L1_ffn_ref(X, routing_W, expert_bias, sW1, sb1, sW2, sb2, rW1, rb1, rW2, rb2):
        import jax, jax.numpy as jnp
        import numpy as np
        E = 8
        K = 2
        B, T, d = X.shape
        shared = jax.nn.silu(X @ sW1 + sb1) @ sW2 + sb2
        logits = jnp.einsum('btd,ed->bte', X, routing_W) + expert_bias
        activation = jnp.sqrt(jax.nn.softplus(logits))
        top_vals, top_idx = jax.lax.top_k(activation, K)
        combine = jnp.sum(jax.nn.one_hot(top_idx, E, dtype=X.dtype) * top_vals[..., None], axis=-2)
        Xf = X.reshape(-1, d)
        cf = combine.reshape(-1, E)
        hdn = jax.nn.silu(jnp.einsum('nd,edh->enh', Xf, rW1) + rb1[:, None, :])
        y = jnp.einsum('enh,ehd->end', hdn, rW2) + rb2[:, None, :]
        routed = jnp.einsum('ne,end->nd', cf, y).reshape(B, T, d)
        return shared + routed
    x = _layernorm(x + _L0_attn_ref(x, L0_attn_wq, L0_attn_wk, L0_attn_wv, L0_attn_wo, L0_attn_head_dirs, L0_attn_scale), axis=-1)
    x = _layernorm(x + _L0_xattn_ref(x, ctx_768, L0_xattn_Wq, L0_xattn_bq, L0_xattn_Wk, L0_xattn_bk, L0_xattn_Wv, L0_xattn_bv, L0_xattn_Wo, L0_xattn_bo), axis=-1)
    x = _layernorm(x + _L0_ffn_ref(x, L0_ffn_k0, L0_ffn_k1, L0_ffn_k2, L0_ffn_s0, L0_ffn_s1, L0_ffn_s2), axis=-1)
    x = _layernorm(x + _L1_attn_ref(x, L1_attn_Wq, L1_attn_Wk, L1_attn_Wv, L1_attn_Wpost), axis=-1)
    x = _layernorm(x + _L1_xattn_ref(x, ctx_768, L1_xattn_Wq, L1_xattn_Wk, L1_xattn_Wv, L1_xattn_Wout, L1_xattn_bout), axis=-1)
    x = _layernorm(x + _L1_ffn_ref(x, L1_ffn_routing_W, L1_ffn_expert_bias, L1_ffn_sW1, L1_ffn_sb1, L1_ffn_sW2, L1_ffn_sb2, L1_ffn_rW1, L1_ffn_rb1, L1_ffn_rW2, L1_ffn_rb2), axis=-1)
    return x

_drawn_inputs = setup_inputs


def setup_inputs(seed=0):
    import zlib

    import numpy as np

    out = dict(_drawn_inputs(seed))
    spreads = {'L0_xattn_bq': (0.0, 0.296),
     'L0_xattn_bk': (0.0, 0.8),
     'L0_xattn_bv': (0.0, 0.1),
     'L0_xattn_bo': (0.0, 0.1),
     'L1_ffn_expert_bias': (0.0, 0.1),
     'L1_ffn_sb1': (0.0, 0.777),
     'L1_ffn_sb2': (0.0, 0.1),
     'L1_ffn_rb1': (0.0, 0.498),
     'L1_ffn_rb2': (0.0, 0.1)}
    factors = {'L1_attn_Wq': 8.0, 'L1_attn_Wk': 8.0, 'L1_xattn_bout': 3.454}
    for name, (base, spread) in spreads.items():
        noise = np.random.default_rng([zlib.crc32(name.encode()), seed]).standard_normal(out[name].shape)
        drawn = base * np.exp(spread * noise) if base else spread * noise
        out[name] = jnp.asarray(drawn.astype(out[name].dtype))
    for name, factor in factors.items():
        out[name] = (out[name] * factor).astype(out[name].dtype)
    return out
```

```python
from contextlib import ExitStack

import numpy as np
import concourse.bass as bass
from concourse import mybir

F32 = mybir.dt.float32
F32R = mybir.dt.float32r
BF16 = mybir.dt.bfloat16
U8 = mybir.dt.uint8
I32 = mybir.dt.int32
ALU = mybir.AluOpType
ACT = mybir.ActivationFunctionType
AX = mybir.AxisListType

B, T, C = 2, 512, 256
TT = T // 128
NKV, CC = 1024, 192
EPS = 1e-5
CLAMP = 10000.0
NEG = -1e30
LAYERS = {
    "A0": dict(H=16, G=4, HT=2, NK=T, D=16),
    "X0": dict(H=16, G=4, HT=1, NK=NKV, D=16),
    "A1": dict(H=16, G=2, HT=2, NK=T, D=64),
    "X1": dict(H=8, G=2, HT=1, NK=NKV, D=64),
}
DMA_LAG = 9
LAG = 2
NP_SLOTS = 3
STACKS = {"X0": 4, "A1": 2, "X1": 2}
NC, NC1 = 5, 7
FFN = 1024
NE = 8
MH = 128
LAST = {"A0": 3, "X0": 3, "A1": 7, "X1": 3}




class Schedule:

    def __init__(self):
        self.steps, self.count, self.at = [], {}, {}
        self.now, self.when = 0, {}

    def add(self, kind, *key):
        self.count[kind] = self.count.get(kind, 0) + 1
        assert (kind, key) not in self.at, (kind, key)
        self.at[(kind, key)] = self.count[kind]
        self.when[(kind, key)] = self.now
        self.steps.append((kind, key))

    def nth(self, kind, *key):
        return self.at[(kind, key)]


def attention_tiles(L, b):
    p = LAYERS[L]
    return [(L, b, g, i, k) for g in range(p["H"] // p["G"]) for i in range(TT)
            for k in range(p["G"] // p["HT"])]


def parts(L):
    return 2 if LAYERS[L]["NK"] > T else 1


def tile_facts(tile):
    L, b, g, i, k = tile
    p = LAYERS[L]
    first = g * p["G"] + k * p["HT"]
    width = (i + 1) * 128 if L == "A0" else min(p["NK"], T)
    return first, p["HT"], width



def turned_by(L, m, half):
    to_act = half == 0 or (L == "X0" and m % 2 == 1) or (L == "A1" and m % 4 == 1)
    return "VA" if to_act else "VD"


def emptied_by(u):
    kind = u[0]
    if kind in ("q", "k"):
        return ("UA", "UD")
    if kind in ("xT", "wo", "f2", "mr", "mb", "my", "dt", "mv", "nf") or (kind == "v" and u[1] == "X0"):
        return ("UD",)
    return ("UA",)


def wide(u):
    return u[0] in ("f0", "f1", "f2", "mr", "mh", "mc", "mb", "my")


def stream(sched, tiles, chains):
    pending = []
    heads = [list(c) for c in chains]
    second_part = []
    late = []
    owed = []

    def empty():
        while pending:
            u = pending.pop(0)
            for kind in emptied_by(u):
                sched.add(kind, *u)

    def ready(item, n):
        return item[0] <= n and all(
            a in sched.at and sched.now - sched.when[a] >= (DMA_LAG if a[1][0] == "X0" and a[0] in ("DS", "DK") else 0)
            for a in item[2])

    def last_of_group(tile):
        L, _, _, i, k = tile
        return i == TT - 1 and k == LAYERS[L]["G"] // LAYERS[L]["HT"] - 1

    n = 0
    while n < len(tiles) + LAG + 1 or any(heads) or pending or owed or late or second_part:
        if n < len(tiles):
            if n == 0:
                sched.add("S", *tiles[0])
                sched.add("M", *tiles[0])
                sched.add("S", *tiles[1])
            if n + 1 < len(tiles):
                sched.add("M", *tiles[n + 1])
            sched.add("E", *tiles[n])
        if 0 <= n - 1 < len(tiles) and tiles[n - 1][0] == "X0":
            sched.add("CL", *tiles[n - 1])
        m = n - LAG
        if 0 <= m < len(tiles):
            for half in range(2):
                sched.add("T", *tiles[m], half)
                sched.add(turned_by(tiles[m][0], m, half), *tiles[m], half)
        if n + 2 < len(tiles):
            L, b, g = tiles[n + 2][:3]
            pair = {"A0": 0, "X0": 2 * g + tiles[n + 2][4] // 2}.get(L, g)
            assert ("DS", (L, b, pair)) in sched.at, tiles[n + 2]
            sched.add("S", *tiles[n + 2])
        if second_part:
            sched.add("AV", *second_part.pop(0))
        while late:
            sched.add(*late.pop(0))
        empty()
        if owed and owed[0][0] == "ON":
            sched.add(*owed.pop(0))
        m = n - LAG - 1
        if 0 <= m < len(tiles):
            L, b, g, i, k = tiles[m]
            if k == LAYERS[L]["G"] // LAYERS[L]["HT"] - 1:
                sched.add("AV", L, b, g, i, 0)
                if parts(L) == 2:
                    second_part.append((L, b, g, i, 1))
                if i == TT - 1 and L == "X0":
                    late.append(("DN", L, b, g))
                    owed += [("UP", "dt", L, b, g), ("UP", "rb", L, b, g), ("ON", L, b, g)]
                elif i == TT - 1:
                    late.append(("ON", L, b, g))
        placed = False
        if owed and not late and not second_part:
            u = owed.pop(0)[1:]
            sched.add("UP", *u)
            pending.append(u)
            placed = True
        if 0 <= n - 1 < len(tiles) and last_of_group(tiles[n - 1]) and tiles[n - 1][0] != "X0":
            group = tiles[n - 1][:3]
            sched.add("RC", *group)
            sched.add("UP", "rb", *group)
            pending.append(("rb", *group))
            placed = True
        moved, held = True, []
        while moved:
            moved = False
            for c in heads:
                while c and c not in held and ready(c[0], n) and not (c[0][1][0] == "unit" and placed):
                    step = c.pop(0)[1]
                    if step[0] == "unit":
                        sched.add("UP", *step[1:])
                        pending.append(step[1:])
                        placed = True
                    else:
                        sched.add(*step)
                        if step[0] in ("LS", "LP"):
                            held.append(c)
                    moved = True
        n += 1
        sched.now += 1
        assert n < 10000, [c[0] for c in heads if c]


def unit(*u, after=(), at=0):
    return (at, ("unit", *u), tuple(after))


def step(*s, after=(), at=0):
    return (at, s, tuple(after))


def UD(*u):
    return ("UD", u)


def UA(*u):
    return ("UA", u)


def after_attention(L, b, nxt):
    last = ("ON", (L, b, LAYERS[L]["H"] // LAYERS[L]["G"] - 1))
    out = [step("GN", b, after=[last, UD("nf")])] if L == "X0" else []
    out += [unit("wo", L, b, 0, after=[last]),
            unit("wo", L, b, 1),
            step("LS", L, b, after=[UD("wo", L, b, 1)]), step("LP", L, b), step("LN", L, b),
            unit("xT", L, b, 0), unit("xT", L, b, 1)]
    if nxt:
        out.append(step("BA", nxt, b, after=[UD("xT", L, b, 1)]))
    return out


def build_schedule():
    sched = Schedule()
    splits = []

    def x0_splits(b, o, after):
        out = []
        for u in (("k", "X0", b, o, 0), ("k", "X0", b, o, 1), ("q", "X0", b, o)):
            a = list(after) if u[0] == "q" else []
            if len(splits) >= NC:
                v = splits[len(splits) - NC]
                a.append(("DK" if v[:2] == ("k", "X0") else "DS", last_user[v]))
            splits.append(u)
            last_user[u] = ("X0", b, 4 * o + 3)
            if u[0] == "q" and (b, o) == (0, 0):
                out += stacked("DK", b, o, [UD("k", "X0", b, o, 1), UA("cT", 3, 1)])
            out.append(unit(*u, after=a))
        kinds = ("DS",) if (b, o) == (0, 0) else ("DK", "DS")
        pairs = [stacked(kind, b, o, [UD("q", "X0", b, o)]) for kind in kinds]
        return out + [item for pair in zip(*pairs) for item in pair]

    def stacked(kind, b, o, after):
        out = []
        for p in range(4 * o, 4 * o + 4):
            P = 8 * b + p
            at = 64 + 16 * (P // 2 - 1) if P >= STACKS["X0"] else 0
            out.append(step(kind, "X0", b, p, at=at, after=after))
        return out

    last_user = {}
    for b in range(B):
        splits.append(("q", "A0", b, 0))
        last_user[splits[-1]] = ("A0", b, 0)

    def a0_start(b):
        return [unit("xT", "in", b, 0), unit("xT", "in", b, 1),
                unit("q", "A0", b, 0, after=[UD("xT", "in", b, 1)]),
                step("DS", "A0", b, 0, after=[UD("q", "A0", b, 0)]),
                unit("v", "A0", b, 0), unit("v", "A0", b, 1)]

    def masked(b, g, at):
        return step("QD" if 4 * b + g < 2 else "QM", b, g, at=at, after=[("DS", ("A0", b, 0))])

    stream(sched, [], [a0_start(0), [masked(0, 0, 0), masked(0, 1, 0)]])
    tiles = [t for L in ("A0", "X0") for b in range(B) for t in attention_tiles(L, b)]
    turned_x = {b: [UD("xT", "A0", b, 1)] for b in range(B)}
    FF = FFN // 128
    scored = ("AV", (*tiles[-1][:4], 1))
    one = [step("XA", 0, after=[scored, UD("xT", "X0", 0, 1)]), step("XD", 0), step("FW", 0)]
    for o in range(FF):
        one += [unit("f0", 0, o), step("FW", 1 + o), step("FS", 0, 0, o, after=[UA("f0", 0, o)])]
    one.append(step("FW", FF + 1))
    for o in range(FF):
        one += [unit("f1", 0, o), step("FS", 1, 0, o, after=[UA("f1", 0, o)])]
    one += [step("XA", 1, after=[UD("xT", "X0", 1, 1)]), step("XD", 1)]
    for o in range(FF):
        one += [unit("f0", 1, o), step("FS", 0, 1, o, after=[UA("f0", 1, o)])]
    one += [unit("f2", 0, hf) for hf in range(2)]
    for o in range(FF):
        one += [unit("f1", 1, o), step("FS", 1, 1, o, after=[UA("f1", 1, o)])]
        one += {2: [step("LS", "F", 0), step("LP", "F", 0)], 3: [step("LN", "F", 0)],
                4: [unit("xT", "F", 0, 0)], 5: [unit("xT", "F", 0, 1)]}.get(o, [])
    one += [unit("f2", 1, hf) for hf in range(2)]
    one += [step("LS", "F", 1, after=[UD("f2", 1, 1)]), step("LP", "F", 1), step("LN", "F", 1),
            unit("xT", "F", 1, 0), unit("xT", "F", 1, 1)]

    chains = [
        [masked(G // 4, G % 4, 8 * (G - 1)) for G in range(2, 8)],
        a0_start(1),
        [unit("cT", sg, c) for sg in range(4) for c in range(2)]
        + x0_splits(0, 0, turned_x[0]) + x0_splits(0, 1, turned_x[0])
        + x0_splits(1, 0, turned_x[1]) + x0_splits(1, 1, turned_x[1]),
        after_attention("A0", 0, "X0"),
        after_attention("A0", 1, "X0"),
        [unit("v", "X0", b, j, at=(12, 44)[b], after=[UA("cT", 3, 1)]) for b in range(B) for j in range(4)] + [unit("mv", at=60)],
        [step("NF", after=[("E", tiles[-1])]), unit("nf")],
        after_attention("X0", 0, None),
        after_attention("X0", 1, None),
        one,
    ]
    stream(sched, tiles, chains)
    splits_of = [splits]

    tiles1 = tiles
    tiles = [t for L in ("A1", "X1") for b in range(B) for t in attention_tiles(L, b)]
    splits = []
    splits_of.append(splits)

    def split_unit(*u, user, after=()):
        a = list(after)
        if len(splits) >= NC1:
            a.append(("DS", last_user[splits[len(splits) - NC1]]))
        splits.append(u)
        last_user[u] = user
        return unit(*u, after=a)

    def starts(P):
        return 4 * P if P < 16 else 64 + 8 * (P - 16)

    def a1_pair(b, p):
        out = []
        if p % 4 == 0:
            out.append(split_unit("k", "A1", b, p // 4, 0, user=("A1", b, p + 3)))
        out.append(split_unit("q", "A1", b, p, user=("A1", b, p)))
        P = 8 * b + p
        out.append(step("DS", "A1", b, p, at=starts(P - 1) - 2 if P > 1 else 0, after=[UD("q", "A1", b, p)]))
        return out

    def x1_keys(b, p):
        return [split_unit("k", "X1", b, p, s, user=("X1", b, p)) for s in range(2)]

    def x1_pair(b, p):
        me = ("X1", b, p)
        P = 16 + 4 * b + p
        out = [] if (b, p) == (0, 0) else x1_keys(b, p)
        after_pair = [] if 4 * b + p < 2 else [("AV", ("X1", *divmod(4 * b + p - 2, 4), TT - 1, 1))]
        out += [split_unit("q", "X1", b, p, user=me, after=[UD("xT", "A1", b, 1)]),
                step("DS", *me, at=starts(P - 1) - 2, after=[UD("q", *me)])]
        out += [unit("v", "X1", b, 2 * p + hf, after=after_pair) for hf in range(2)]
        return out

    stream(sched, [], [a1_pair(0, 0) + a1_pair(0, 1) + [unit("v", "A1", 0, j) for j in range(2)]])
    def experts(b):
        scored = ("AV", (*tiles[-1][:4], 1))
        stages = [step("ZD", b, 0, after=[UD("mr", b)]), step("ZA", b, 0), step("ZD", b, 1), step("ZP", b),
                  step("ZD", b, 2), unit("mc", b)]
        out = [unit("mr", b, after=[scored, UD("xT", "X1", b, 1)])]
        for e in range(NE + 1):
            out += stages[e - 1:e] if e else []
            out.append(unit("mh", b, e, after=[("UP", ("mr", b))]))
        out += [unit("mb", b, e, after=[UA("mc", b)]) for e in range(NE)]
        out += [unit("my", b, 0), unit("my", b, 1), step("LS", "M", b, after=[UD("my", b, 1)]),
                step("LP", "M", b), step("LN", "M", b)]
        return out

    pairs = []
    for P in range(2, 16):
        if P == 15:
            pairs += x1_keys(0, 0)
        pairs += a1_pair(P // 8, P % 8)
    for P in range(8):
        pairs += x1_pair(P // 4, P % 4)
    chains = [
        after_attention("A1", 0, "X1"),
        pairs,
        [unit("v", "A1", 1, j) for j in range(2)],
        after_attention("A1", 1, "X1"),
        after_attention("X1", 0, None), after_attention("X1", 1, None),
        experts(0), experts(1),
    ]
    stream(sched, tiles, chains)

    return sched, splits_of, last_user, [tiles1, tiles]


def decoder(nc, d, out):
    sched, splits_of, last_user, phases = build_schedule()
    nth = sched.nth
    tile_no = {t: n for tiles in phases for n, t in enumerate(tiles)}
    all_tiles = [t for tiles in phases for t in tiles]

    def tile_back(t, k):
        i = all_index[t] - k
        return all_tiles[i] if i >= 0 else None
    all_index = {t: i for i, t in enumerate(all_tiles)}
    unit_order = [key for kind, key in sched.steps if kind == "UP"]
    narrow = [u for u in unit_order if not wide(u)]
    broad = [u for u in unit_order if wide(u)]
    unit_before = {u: (narrow[i - 1] if i else None) for i, u in enumerate(narrow)}
    unit_before |= {u: (broad[i - 4] if i >= 4 else None) for i, u in enumerate(broad)}
    bank_no = {u: i % 4 for i, u in enumerate(broad)}
    groups = [key for kind, key in sched.steps if kind == "ON"]
    place_of, place_before = {}, {}
    for places, splits in zip((NC, NC1), splits_of):
        for i, u in enumerate(splits):
            place_of[u] = i % places
            place_before[u] = splits[i - places] if i >= places else None

    ctx = ExitStack()
    with ctx:
        def sem(name):
            return ctx.enter_context(nc.semaphore(name))

        def sb(name, shape, dt=F32, into=None):
            return (into or ctx).enter_context(nc.sbuf_tensor(name, shape, dt))

        def ps(name, shape):
            return ctx.enter_context(nc.psum_tensor(name, shape, F32))

        p_scores = ps("p_scores", [128, 2, 1024])
        p_turn = ps("p_turn", [128, 2, 512])
        p_out = ps("p_out", [128, 512])
        p_unit = ps("p_unit", [128, 512])

        x = sb("x", [128, B * TT, C])
        xT = sb("xT", [128, 2, B * T])
        ctxT0 = sb("ctxT0", [128, B * NKV])
        ctxT1 = sb("ctxT1", [CC - 128, B * NKV])
        ident = sb("ident", [128, 128])
        stats = sb("stats", [128, B * TT, 6])
        mv = sb("mv", [128, B * TT, 2])
        veps = sb("veps", [128, B * TT])
        rstd = sb("rstd", [128, B * TT])
        minus_half = sb("minus_half", [128, B * TT])
        nmax = sb("nmax", [128, 4, 2])
        sums = sb("sums", [128, 2, TT, 4])
        rsum = sb("rsum", [128, 2, TT, 4])
        rwide = sb("rwide", [128, TT, 128])
        spread = sb("spread", [128, 512])

        first = ExitStack()
        arriving = ExitStack()
        ctx_raw = sb("ctx_raw", [128, B * NKV // 128, CC], into=arriving)
        arriving.close()
        x0_ks = sb("x0_ks", [128, STACKS["X0"], NKV], F32R, into=first)
        VW = 272
        a0_v = sb("a0_v", [128, B, TT, VW], into=first)
        a0_qs = sb("a0_qs", [128, B, 2, T], F32R, into=first)
        a0_ks = sb("a0_ks", [128, B, 2, T], F32R, into=first)
        masked = ExitStack()
        a0_qm = sb("a0_qm", [128, 8, T], F32R, into=masked)
        masked.close()
        outT_x = sb("outT_x", [128, B, 4, T], into=first)
        outT_a = sb("outT_a", [128, 4, T], into=first)
        PT_A = 5
        x0_raw = outT_a[:, 0, :]
        x0_nans = outT_a[:, 1, 0:128]
        wo_rows = sb("wo_rows", [128, 4, C], into=first)
        x0_sums = sb("x0_sums", [128, B, 4, TT, 4], into=first)
        x0_nan = sb("x0_nan", [128, 2], into=first)
        ones = sb("ones", [128, 128], into=first)
        x0_mean = sb("x0_mean", [128, B, 4], into=first)
        prob_a = sb("prob_a", [128, NP_SLOTS, 1024], into=first)
        splitH_a = sb("splitH_a", [128, NC, 512], F32R, into=first)
        splitL_a = sb("splitL_a", [128, NC, 512], F32R, into=first)
        probT_a = sb("probT_a", [128, PT_A, 8, 128], into=first)
        identb = sb("identb", [128, 128], BF16, into=first)
        hidden = sb("hidden", [128, 128], BF16, into=first)
        head_rows = sb("head_rows", [128, 8], into=first)
        a0_raw = sb("a0_raw", [128, 2, 2, 48], into=first)
        a0_dirs = sb("a0_dirs", [128, 48], into=first)
        a0_tmp = sb("a0_tmp", [128, 48], into=first)
        a0_scale = sb("a0_scale", [128, 1], into=first)
        a0_wqk = sb("a0_wqk", [128, 2, 128], into=first)
        a0_wv = sb("a0_wv", [128, 2, C], into=first)
        x0_wq = sb("x0_wq", [128, 2, C], into=first)
        x0_wk0 = sb("x0_wk0", [128, C], into=first)
        x0_wk1 = sb("x0_wk1", [CC - 128, C], into=first)
        x0_wv0 = sb("x0_wv0", [128, C + 16], into=first)
        x0_wv1 = sb("x0_wv1", [CC - 128, C + 16], into=first)
        x0_bq = sb("x0_bq", [128, 2], into=first)
        x0_bk = sb("x0_bk", [128, 2], into=first)
        x0_bv = sb("x0_bv", [128, C], into=first)
        x0_bo = sb("x0_bo", [128, C], into=first)
        VX = 288
        x0_v = sb("x0_v", [128, B, NKV // 128, VX], into=first)
        x0_lo = sb("x0_lo", [128, 4], into=first)
        minus_clamp = sb("minus_clamp", [128, 1], into=first)
        ctx_sum0 = sb("ctx_sum0", [128, 4], into=first)
        ctx_sum1 = sb("ctx_sum1", [CC - 128, 4], into=first)
        x0_bvT = sb("x0_bvT", [128, 4], into=first)
        x0_qs = sb("x0_qs", [128, STACKS["X0"], 2, T], F32R, into=first)
        first.close()

        second = ExitStack()
        a1_weights = ExitStack()
        a1_wq = sb("a1_wq", [128, 2, 1024], into=a1_weights)
        a1_wk = sb("a1_wk", [128, 2, C], into=a1_weights)
        a1_wv = sb("a1_wv", [128, 2, C], into=a1_weights)
        a1_wo = sb("a1_wo", [128, 8, C], into=a1_weights)
        a1_weights.close()
        m_w1 = sb("m_w1", [128, NE + 1, 2, MH], into=second)
        m_w2 = sb("m_w2", [128, NE + 1, C], into=second)
        m_b1 = sb("m_b1", [128, NE + 1], into=second)
        m_b2 = sb("m_b2", [NE + 1, C], into=second)
        m_wr = sb("m_wr", [128, 2, NE], into=second)
        m_br = sb("m_br", [128, NE], into=second)
        m_lt = sb("m_lt", [128, NE, NE], into=second)
        half_up = sb("half_up", [128, TT, NE], into=second)
        m_gate = sb("m_gate", [128, B, TT, NE + 1], into=second)
        m_z = sb("m_z", [128, B, 8, TT, NE], into=second)

        network = ExitStack()
        k0_words = sb("k0_words", [128, 4, FFN // 4], I32, into=network)
        k1_words = sb("k1_words", [128, FFN // 128, FFN // 4], I32, into=network)
        k2_words = sb("k2_words", [128, FFN // 128, C // 4], I32, into=network)
        h1H = sb("h1H", [128, FFN // 128, T], F32R, into=network)
        h1L = sb("h1L", [128, FFN // 128, T], F32R, into=network)
        k2 = sb("k2", [128, FFN // 128, C], F32R, into=network)
        k0 = sb("k0", [128, 2, FFN], F32R, into=network)
        k1 = sb("k1", [128, FFN // 128, FFN], F32R, into=network)
        xTH = sb("xTH", [128, 2, T], F32R, into=network)
        xTL = sb("xTL", [128, 2, T], F32R, into=network)
        hH = [sb("h0H", [128, FFN // 128, T], F32R, into=network), h1H]
        hL = [sb("h0L", [128, FFN // 128, T], F32R, into=network), h1L]
        relu = sb("relu", [128, 2, T], into=network)
        f_scale = sb("f_scale", [128, 3], into=network)
        network.close()

        PT_B = 4
        attention = ExitStack()
        prob_b = sb("prob_b", [128, NP_SLOTS, 1024], into=attention)
        splitH_b = sb("splitH_b", [128, NC1, 512], F32R, into=attention)
        splitL_b = sb("splitL_b", [128, NC1, 512], F32R, into=attention)
        probT_b = sb("probT_b", [128, PT_B, 8, 128], into=attention)
        outT_b = sb("outT_b", [128, 8, T], into=attention)
        stacks = sb("stacks", [128, 2, 10 * 512], F32R, into=attention)
        a1_v = sb("a1_v", [128, B, TT, C], into=attention)
        x1_v = sb("x1_v", [128, 2, NKV // 128, 128], into=attention)
        x1_wq = sb("x1_wq", [128, 2, 512], into=attention)
        x1_wk0 = sb("x1_wk0", [128, 512], into=attention)
        x1_wk1 = sb("x1_wk1", [CC - 128, 512], into=attention)
        x1_wv0 = sb("x1_wv0", [128, 512], into=attention)
        x1_wv1 = sb("x1_wv1", [CC - 128, 512], into=attention)
        x1_wo = sb("x1_wo", [128, 4, C], into=attention)
        x1_bo = sb("x1_bo", [128, C], into=attention)
        attention.close()

        m_h = sb("m_h", [128, B, NE + 1, T], into=second)
        m_cmp = sb("m_cmp", [128, 3, TT, NE, NE], into=second)
        m_gateT = sb("m_gateT", [NE + 1, B, T], into=second)
        second.close()

        def by_layer(L, a, b):
            return a if L in ("A0", "X0") else b

        names = {
            "S": "scores_ready", "M": "max_ready", "E": "probs_ready", "T": "probs_turned",
            "VA": "turned_kept_by_act", "VD": "turned_kept_by_dve", "AV": "outputs_added",
            "RC": "sums_inverted", "ON": "outputs_scaled", "UP": "unit_ready",
            "UA": "unit_emptied_by_act", "UD": "unit_emptied_by_dve", "QM": "queries_masked", "QD": "first_queries_masked",
            "BA": "bias_added", "LS": "variances_ready", "LP": "deviations_inverted",
            "LN": "x_normalised", "XA": "x_rounded", "XD": "x_rest_ready", "FW": "signs_ready",
            "FS": "hidden_split", "CL": "probs_clipped", "DN": "outputs_kept", "NF": "nans_counted", "GN": "nans_replaced",
            "ZD": "gates_by_dve", "ZA": "gates_by_act", "ZP": "roots_ready",
        }
        done = {k: sem(v) for k, v in names.items()}
        a0_stacked = [sem(f"a0_stacked{b}") for b in range(B)]
        pair_stacked = [sem(f"pair_stacked{s}") for s in range(2)]
        x0_keys_stacked = [sem(f"x0_keys_stacked{s}") for s in range(STACKS["X0"])]
        x0_queries_stacked = [sem(f"x0_queries_stacked{s}") for s in range(STACKS["X0"])]
        x_loaded, ctx_loaded = sem("x_loaded"), sem("ctx_loaded")
        a0_loaded, a0w_loaded, x0_loaded = sem("a0_loaded"), sem("a0w_loaded"), sem("x0_loaded")
        consts_ready = sem("consts_ready")
        wo_cleared = sem("wo_cleared")
        wqk_ready, heads_marked = sem("wqk_ready"), sem("heads_marked")
        x0_scaled, x0_wo_loaded = sem("x0_scaled"), sem("x0_wo_loaded")
        signs_loaded, f_scales_loaded, f_scaled = sem("signs_loaded"), sem("f_scales_loaded"), sem("f_scaled")
        a1_loaded, a1_scaled, x1_loaded, x1_scaled = (sem(n) for n in ("a1_loaded", "a1_scaled", "x1_loaded", "x1_scaled"))
        m_loaded, m_consts = sem("m_loaded"), sem("m_consts")
        act_chain = sem("act_chain")
        out_stored = sem("out_stored")
        dve_chain, pool_chain = sem("dve_chain"), sem("pool_chain")

        def wait(eng, kind, *key):
            eng.wait_ge(done[kind], nth(kind, *key))

        A0_DMAS, X0_DMAS = 16, 8
        pair_key = {}
        pair_count = {}
        for P in range(24):
            key = ("A1", P // 8, P % 8) if P < 16 else ("X1", (P - 16) // 4, P % 4)
            dmas = 8 if P < 16 else 20
            pair_count[key] = 16 * dmas + (pair_count[pair_key[P - 2]] if P >= 2 else 0)
            pair_key[P] = key

        both = (x0_keys_stacked, x0_queries_stacked)

        def stack_whole(eng, L, b, p, kinds=both):
            if L == "A0":
                eng.wait_ge(a0_stacked[b], 16 * A0_DMAS)
            elif L == "X0":
                P = b * 8 + p
                for kind in kinds:
                    eng.wait_ge(kind[P % 4], 16 * X0_DMAS * (P // 4 + 1))
            else:
                eng.wait_ge(pair_stacked[pair_no(L, b, p) % 2], pair_count[(L, b, p)])

        def pair_no(L, b, p):
            return 8 * b + p if L == "A1" else 16 + 4 * b + p

        def bank(u):
            if not wide(u):
                return p_unit
            r = bank_no[u]
            return p_scores[:, r // 2, 512 * (r % 2):512 * (r % 2) + 512]

        def bank_free(eng, u):
            v = unit_before[u]
            if v is not None:
                for kind in emptied_by(v):
                    wait(eng, kind, *v)

        def place_free(eng, u):
            v = place_before[u]
            if v is not None:
                stack_whole(eng, *last_user[v], kinds=both[0:1] if v[0] == "k" else both[1:2])

        def attentions_over(eng):
            wait(eng, "AV", *phases[0][-1][:4], 1)
            wait(eng, "BA", "X0", 1)

        def mask_queries(eng, b, g):
            for h in range(4 * g, 4 * g + 4):
                ins = eng.tensor_scalar(a0_qm[:, (16 * b + h) % 8], a0_qs[:, b, h // 8].bitcast(F32),
                                        head_rows[:, h % 8:h % 8 + 1], None, ALU.mult)
            return ins

        def tokens(b, i):
            return b * TT + i

        group_no = {g: i for i, g in enumerate(groups)}

        def turned_bank_free(eng, t, half):
            v = tile_back(t, 1)
            if v:
                wait(eng, turned_by(v[0], tile_no[v], half), *v, half)

        def blocks_of(key, half):
            L, b, g, i, k = key
            return range(4 * half, 4 * half + (i + 1 if L == "A0" else 4))

        def keep_turned(eng, key, copy):
            *t, half = key
            t = tuple(t)
            n = tile_no[t]
            wait(eng, "T", *t, half)
            L = t[0]
            places, probT = by_layer(L, PT_A, PT_B), by_layer(L, probT_a, probT_b)
            v = tile_back(t, places)
            if v:
                wait(eng, "AV", *v[:4], half if parts(v[0]) == 2 else 0)
            bl = blocks_of(t, half)
            m = len(bl)
            return copy(probT[:, n % places, bl[0]:bl[0] + m, :],
                        p_turn[:, half, 0:128 * m].rearrange("p (j t) -> p j t", j=m))

        def keys_turned(eng, sg):
            wait(eng, "UA", "cT", sg, 1)

        def values_ready(eng, L, b, g):
            if L in ("A0", "A1"):
                wait(eng, "UA", "v", L, b, 1)
            elif L == "X0":
                wait(eng, "UD", "v", L, b, 3)
            else:
                wait(eng, "UA", "v", L, b, 2 * g + 1)

        def values(L, b, h, j):
            if L == "A0":
                return a0_v[:, b, j, 16 * h:16 * h + 32]
            if L == "X0":
                return x0_v[:, b, j, 17 * h:17 * h + 32]
            if L == "A1":
                return a1_v[:, b, j, 64 * (h // 4):64 * (h // 4) + 64]
            return x1_v[:, (4 * b + h // 2) % 2, j, 64 * (h % 2):64 * (h % 2) + 64]

        layer_batches = []
        for L, b, g in groups:
            if (L, b) not in layer_batches:
                layer_batches.append((L, b))
        prev_batch = {lb: (layer_batches[i - 1] if i else None) for i, lb in enumerate(layer_batches)}

        relu_units = [u for u in unit_order if u[0] in ("f0", "f1")]
        relu_no = {u: i for i, u in enumerate(relu_units)}

        def relu_key(u):
            return (int(u[0] == "f1"), u[1], u[2])

        block = ctx.enter_context(nc.Block())

        @block.sync
        def _(sp):
            def rows(name):
                return d[name].rearrange("(c p) n -> p c n", p=128)

            for j, n in enumerate(("L0_attn_wq", "L0_attn_wk")):
                sp.dma_start(a0_raw[:, j], rows(n)).then_inc(a0_loaded, 16)
            sp.dma_start(a0_dirs[:, :], d["L0_attn_head_dirs"].rearrange("h d -> (h d)")
                         .partition_broadcast(128)).then_inc(a0_loaded, 16)
            sp.dma_start(a0_scale[:, :], d["L0_attn_scale"].partition_broadcast(128)).then_inc(a0_loaded, 16)
            sp.dma_start(a0_wv[:, :, :], rows("L0_attn_wv")).then_inc(a0w_loaded, 16)
            sp.dma_start(x0_wq[:, :, :], rows("L0_xattn_Wq")).then_inc(x0_loaded, 16)
            for w0, w1, n in ((x0_wk0, x0_wk1, "L0_xattn_Wk"), (x0_wv0, x0_wv1, "L0_xattn_Wv")):
                sp.dma_start(w0[:, 0:C], d[n][0:128, :]).then_inc(x0_loaded, 16)
                sp.dma_start(w1[:, 0:C], d[n][128:CC, :]).then_inc(x0_loaded, 16)
            for t, n in ((x0_bq, "L0_xattn_bq"), (x0_bk, "L0_xattn_bk")):
                sp.dma_start(t[:, :], d[n].rearrange("(o p) -> p o", p=128), allow_slow_non_contiguous=True).then_inc(x0_loaded, 16)
            for t, n in ((x0_bv, "L0_xattn_bv"), (x0_bo, "L0_xattn_bo")):
                sp.dma_start(t[:, :], d[n].partition_broadcast(128)).then_inc(x0_loaded, 16)
            sp.wait_ge(wo_cleared, 1)
            bv = d["L0_xattn_bv"].rearrange("(g a p) -> a p g", a=4, p=16)
            for a in range(4):
                sp.dma_start(x0_bvT[32 * a:32 * a + 16, :], bv[a], allow_slow_non_contiguous=True).then_inc(x0_loaded, 16)

            def load_wo(name, loaded):
                src = d[name].rearrange("(g a p) n -> a p g n", a=4, p=16)
                for a in range(4):
                    sp.dma_start(wo_rows[32 * a:32 * a + 16, :, :], src[a]).then_inc(loaded, 16)
            load_wo("L0_attn_wo", a0w_loaded)

            def stack(to, of, whole):
                sp.dma_start(to.bitcast(F32), of.bitcast(F32)).then_inc(whole, 16)

            def load_signs():
                wait(sp, "UP", "wo", "A0", 1, 1)
                load_wo("L0_xattn_Wo", x0_wo_loaded)
                wait(sp, "AV", "A0", 1, 3, TT - 1, 0)
                for t, n in ((k0_words, "L0_ffn_k0"), (k1_words, "L0_ffn_k1"), (k2_words, "L0_ffn_k2")):
                    sp.dma_start(t[:, :, :], rows(n)).then_inc(signs_loaded, 16)

            def load_a1():
                attentions_over(sp)
                for j, n in enumerate(("s0", "s1", "s2")):
                    sp.dma_start(f_scale[:, j:j + 1], d["L0_ffn_" + n].partition_broadcast(128),
                                 allow_slow_non_contiguous=True).then_inc(f_scales_loaded, 16)
                for t, n in ((a1_wq, "Wq"), (a1_wk, "Wk"), (a1_wv, "Wv"), (a1_wo, "Wpost")):
                    sp.dma_start(t[:, :, :], rows("L1_attn_" + n)).then_inc(a1_loaded, 16)

            def load_x1():
                wait(sp, "UD", "xT", "F", 1, 1)
                sp.dma_start(x1_wq[:, :, :], rows("L1_xattn_Wq")).then_inc(x1_loaded, 16)
                for w0, w1, n in ((x1_wk0, x1_wk1, "L1_xattn_Wk"), (x1_wv0, x1_wv1, "L1_xattn_Wv")):
                    sp.dma_start(w0[:, :], d[n][0:128, :]).then_inc(x1_loaded, 16)
                    sp.dma_start(w1[:, :], d[n][128:CC, :]).then_inc(x1_loaded, 16)
                sp.dma_start(x1_wo[:, :, :], rows("L1_xattn_Wout")).then_inc(x1_loaded, 16)
                sp.dma_start(x1_bo[:, :], d["L1_xattn_bout"].partition_broadcast(128)).then_inc(x1_loaded, 16)

            def load_experts():
                wait(sp, "UP", "wo", "A1", 1, 1)
                for e in range(NE):
                    sp.dma_start(m_w1[:, e], d["L1_ffn_rW1"][e].rearrange("(c p) h -> p c h", p=128)).then_inc(m_loaded, 16)
                sp.dma_start(m_w1[:, NE], rows("L1_ffn_sW1")).then_inc(m_loaded, 16)
                sp.dma_start(m_w2[:, 0:NE, :], d["L1_ffn_rW2"].rearrange("e h n -> h e n")).then_inc(m_loaded, 16)
                sp.dma_start(m_w2[:, NE, :], d["L1_ffn_sW2"]).then_inc(m_loaded, 16)
                sp.dma_start(m_b1[:, 0:NE], d["L1_ffn_rb1"].rearrange("e h -> h e"), allow_slow_non_contiguous=True).then_inc(m_loaded, 16)
                sp.dma_start(m_b1[:, NE:NE + 1], d["L1_ffn_sb1"].rearrange("(h o) -> h o", o=1), allow_slow_non_contiguous=True).then_inc(m_loaded, 16)
                sp.dma_start(m_b2[0:NE, :], d["L1_ffn_rb2"]).then_inc(m_loaded, 16)
                sp.dma_start(m_b2[NE:NE + 1, :], d["L1_ffn_sb2"].rearrange("(o n) -> o n", o=1)).then_inc(m_loaded, 16)
                for c in range(2):
                    sp.dma_start(m_wr[:, c, :], d["L1_ffn_routing_W"][:, 128 * c:128 * c + 128].rearrange("e p -> p e"),
                                 allow_slow_non_contiguous=True).then_inc(m_loaded, 16)
                sp.dma_start(m_br[:, :], d["L1_ffn_expert_bias"].partition_broadcast(128)).then_inc(m_loaded, 16)

            for kind, key in sched.steps:
                if kind not in ("DS", "DK"):
                    continue
                L, b, p = key
                if (kind, key) == ("DS", ("X0", 1, 0)):
                    load_signs()
                elif key == ("A1", 0, 0):
                    load_a1()
                elif key == ("A1", 0, 2):
                    load_x1()
                elif key == ("X1", 0, 3):
                    load_experts()
                splitH, splitL = by_layer(L, splitH_a, splitH_b), by_layer(L, splitL_a, splitL_b)
                if L == "A0":
                    u = ("q", "A0", b, 0)
                    wait(sp, "UA", *u)
                    wait(sp, "UD", *u)
                    H, Lo = splitH[:, place_of[u]], splitL[:, place_of[u]]
                    for o in range(2):
                        for s in range(4):
                            q, k = (H, Lo)[s % 2], (H, Lo)[s // 2]
                            stack(a0_qs[32 * s:32 * s + 32, b, o], q[32 * o:32 * o + 32], a0_stacked[b])
                            stack(a0_ks[32 * s:32 * s + 32, b, o], k[64 + 32 * o:96 + 32 * o], a0_stacked[b])
                elif L == "X0":
                    P = b * 8 + p
                    slot, o, r = P % 4, p // 4, 32 * (p % 4)
                    for u in ((("k", L, b, o, 0), ("k", L, b, o, 1)) if kind == "DK" else (("q", L, b, o),)):
                        wait(sp, "UA", *u)
                        wait(sp, "UD", *u)
                    if P >= 4:
                        Q = P - 4
                        wait(sp, "S", L, Q // 8, (Q % 8) // 2, TT - 1, 3)
                    else:
                        sp.wait_ge(wo_cleared, 2)
                        wait(sp, "UP", "cT", 3, 1)
                    for s in range(4):
                        if kind == "DS":
                            q = (splitH, splitL)[s % 2][:, place_of[("q", L, b, o)]]
                            for a in range(2):
                                stack(x0_qs[32 * s + 16 * a:32 * s + 16 * a + 16, slot, a],
                                      q[r + 16 * a:r + 16 * a + 16], x0_queries_stacked[slot])
                            continue
                        for h in range(2):
                            k = (splitH, splitL)[s // 2][:, place_of[("k", L, b, o, h)]]
                            stack(x0_ks[32 * s:32 * s + 32, slot, T * h:T * h + T], k[r:r + 32], x0_keys_stacked[slot])
                else:
                    P = pair_no(L, b, p)
                    slot, whole = P % 2, pair_stacked[P % 2]
                    if L == "A1":
                        ks = [("k", L, b, p // 4, 0)]
                    else:
                        ks = [("k", L, b, p, 0), ("k", L, b, p, 1)]
                    for u in [("q", L, b, p)] + ks:
                        wait(sp, "UA", *u)
                        wait(sp, "UD", *u)
                    if P >= 2:
                        Lp, bp, pp = pair_key[P - 2]
                        wait(sp, "S", Lp, bp, pp, TT - 1, 0 if Lp == "A1" else 1)
                    for part in range(2):
                        rows_to = slice(64 * part, 64 * part + 64)
                        for a in range(2):
                            q = (splitH, splitL)[part][:, place_of[("q", L, b, p)]]
                            stack(stacks[rows_to, slot, 512 * a:512 * a + 512], q[64 * a:64 * a + 64], whole)
                    for part in range(2):
                        Kp = (splitH, splitL)[part]
                        for rows_to in (slice(0, 64), slice(64, 128)):
                            if L == "A1":
                                r = 64 * (p // 2 % 2)
                                at = 1024 + 512 * part
                                stack(stacks[rows_to, slot, at:at + 512], Kp[r:r + 64, place_of[ks[0]]], whole)
                                continue
                            for a in range(2):
                                for s in range(2):
                                    at = 1024 + (2 * a + part) * 1024 + 512 * s
                                    stack(stacks[rows_to, slot, at:at + 512],
                                          Kp[64 * a:64 * a + 64, place_of[ks[s]]], whole)

            o = out.rearrange("b (i p) c -> b p i c", p=128)
            for b in range(B):
                wait(sp, "LN", "M", b)
                sp.dma_start(o[b], x[:, b * TT:(b + 1) * TT, :]).then_inc(out_stored, 16)
            sp.wait_ge(out_stored, 16 * B)

        @block.gpsimd
        def _(pool):
            links = [0]

            def link(ins):
                links[0] += 1
                ins.then_inc(pool_chain, 1)
                pool.wait_ge(pool_chain, links[0])

            nc.gpsimd.memset(ident[:, :], 0.0)
            nc.gpsimd.memset(identb[:, :], 0.0)
            nc.gpsimd.memset(hidden[:, :], 0.0)
            nc.gpsimd.memset(minus_half[:, :], -0.5)
            link(nc.gpsimd.memset(head_rows[:, :], 1.0))
            for t in (ident, identb):
                nc.gpsimd.affine_select(out=t[:, :], in_=t[:, :], compare_op=ALU.not_equal, fill=1.0, base=0,
                                        pattern=[[-1, 128]], channel_multiplier=1)
            nc.gpsimd.affine_select(out=hidden[:, :], in_=hidden[:, :], compare_op=ALU.is_ge, fill=NEG,
                                    base=0, pattern=[[-1, 128]], channel_multiplier=1).then_inc(consts_ready, 1)
            for q in range(4):
                t = head_rows[32 * q:32 * q + 32, :]
                link(nc.gpsimd.affine_select(out=t, in_=t, compare_op=ALU.is_ge, fill=0.0, base=0,
                                             pattern=[[-4, 8]], channel_multiplier=1))
                link(nc.gpsimd.affine_select(out=t, in_=t, compare_op=ALU.is_ge, fill=0.0, base=3,
                                             pattern=[[4, 8]], channel_multiplier=-1))
            nc.gpsimd.memset(minus_clamp[:, :], -CLAMP).then_inc(heads_marked, 1)
            nc.gpsimd.memset(x0_bvT[:, :], 0.0)
            nc.gpsimd.memset(wo_rows[:, :, :], 0.0).then_inc(wo_cleared, 1)
            nc.gpsimd.memset(a0_v[:, :, :, 256:VW], 0.0)
            nc.gpsimd.memset(x0_wv0[:, C:], 0.0)
            nc.gpsimd.memset(x0_wv1[:, C:], 0.0)
            nc.gpsimd.memset(x0_v[:, :, :, 272:VX], 0.0)
            nc.gpsimd.memset(ones[:, :], 1.0)
            nc.gpsimd.memset(x0_v[:, :, :, 0:272].rearrange("p b j (h c) -> p (b j) h c", c=17)[:, :, :, 16], 1.0)\
              .then_inc(consts_ready, 1)
            nc.gpsimd.memset(x0_qs[:, :, :, :].bitcast(F32), 0.0).then_inc(wo_cleared, 1)

            def scaled():
                pool.wait_ge(x0_loaded, 16 * 13)
                k = LAYERS["X0"]["D"] ** -0.5
                nc.gpsimd.tensor_scalar(x0_bq[:, :], x0_bq[:, :], k, None, ALU.mult)
                nc.gpsimd.tensor_scalar(x0_wq[:, :, :], x0_wq[:, :, :], k, None, ALU.mult).then_inc(x0_scaled, 1)

            for kind, key in sched.steps:
                if kind == "QM":
                    b, g = key
                    G = 4 * b + g
                    if G == 2:
                        scaled()
                    stack_whole(pool, "A0", b, 0)
                    wait(pool, "S", "A0", (G - 2) // 4, (G - 2) % 4, TT - 1, 1)
                    mask_queries(nc.gpsimd, b, g).then_inc(done["QM"], 1)
                elif kind == "XA" and key == (0,):
                    pool.wait_ge(f_scales_loaded, 48)
                    nc.gpsimd.tensor_scalar(f_scale[:, 0:1], f_scale[:, 0:1], 4.0, None, ALU.mult).then_inc(f_scaled, 1)
                    nc.gpsimd.tensor_scalar(f_scale[:, 1:2], f_scale[:, 1:2], 2.0, None, ALU.mult).then_inc(f_scaled, 1)
                    pool.wait_ge(a1_loaded, 64)
                    nc.gpsimd.tensor_scalar(a1_wq[:, :, :], a1_wq[:, :, :], LAYERS["A1"]["D"] ** -0.5, None, ALU.mult)\
                      .then_inc(a1_scaled, 1)
                elif kind == "DS" and key == ("A1", 0, 2):
                    pool.wait_ge(x1_loaded, 16 * 7)
                    nc.gpsimd.tensor_scalar(x1_wq[:, :, :], x1_wq[:, :, :], LAYERS["X1"]["D"] ** -0.5, None, ALU.mult)\
                      .then_inc(x1_scaled, 1)
                elif kind == "ZP":
                    b, = key
                    wait(pool, "ZD", b, 1)
                    nc.gpsimd.tensor_tensor(m_z[:, b, 1], m_z[:, b, 7], half_up[:, :, :], ALU.pow).then_inc(done["ZP"], 1)
                elif kind == "UP" and key == ("mr", 0):
                    wait(pool, "UP", "wo", "A1", 1, 1)
                    nc.gpsimd.memset(half_up[:, :, :], 0.5)
                    nc.gpsimd.memset(m_gate[:, :, :, :], 1.0)
                    link(nc.gpsimd.memset(m_lt[:, :, :], 1.0))
                    nc.gpsimd.affine_select(out=m_lt[:, :, :], in_=m_lt[:, :, :], compare_op=ALU.is_gt, fill=0.0,
                                            base=0, pattern=[[1, NE], [-1, NE]], channel_multiplier=0)\
                      .then_inc(m_consts, 1)
                elif kind == "BA":
                    L, b = key
                    prev = {"X0": "A0", "X1": "A1"}[L]
                    wait(pool, "UP", "xT", prev, b, 1)
                    bias = {"X0": x0_bo, "X1": x1_bo}[L]
                    xb = x[:, b * TT:(b + 1) * TT, :]
                    nc.gpsimd.tensor_tensor(xb, xb, bias[:, :].unsqueeze(1).to_broadcast([128, TT, C]), ALU.add)\
                      .then_inc(done["BA"], 1)
                elif kind == "LP":
                    L, b = key
                    s = slice(b * TT, (b + 1) * TT)
                    wait(pool, "LS", L, b)
                    link(nc.gpsimd.tensor_scalar(veps[:, s], mv[:, s, 1], EPS, None, ALU.add))
                    nc.gpsimd.tensor_tensor(rstd[:, s], veps[:, s], minus_half[:, s], ALU.pow).then_inc(done["LP"], 1)

        @block.scalar
        def _(act):
            links = [0]

            def link(ins):
                links[0] += 1
                ins.then_inc(act_chain, 1)
                act.wait_ge(act_chain, links[0])

            for b in range(B):
                act.dma_start(x[:, b * TT:(b + 1) * TT, :], d["x"][b].rearrange("(i p) c -> p i c", p=128))\
                   .then_inc(x_loaded, 16)
            act.dma_start(ctx_raw[:, :, :], d["ctx_768"].rearrange("b (i p) c -> p (b i) c", p=128))\
               .then_inc(ctx_loaded, 16)

            for kind, key in sched.steps:
                if kind == "E":
                    L, b, g, i, k = key
                    n = tile_no[key]
                    h0, heads, w = tile_facts(key)
                    wait(act, "M", *key)
                    back = tile_back(key, NP_SLOTS)
                    if back:
                        wait(act, "T", *back, 1)
                    G = group_no[(L, b, g)]
                    if L == "X0":
                        nc.scalar.activation(x0_lo[:, n % 4:n % 4 + 1], nmax[:, n % 4, 0:1], ACT.Exp,
                                             bias=minus_clamp[:, 0:1])
                        sums_to = x0_sums[:, b, g]
                    else:
                        sums_to = sums[:, G % 2]
                        if G >= 2 and groups[G - 2][0] != "X0" and i == 0 and k == 0:
                            wait(act, "RC", *groups[G - 2])
                    for a in range(heads):
                        w_all = w if heads == 2 else LAYERS[L]["NK"]
                        ins = nc.scalar.activation(
                            by_layer(L, prob_a, prob_b)[:, n % NP_SLOTS, a * 512:a * 512 + w_all],
                            p_scores[:, n % 2, a * 512:a * 512 + w_all], ACT.Exp,
                            bias=nmax[:, n % 4, a:a + 1], scale=1.0,
                            accum_out=sums_to[:, i, k * heads + a:k * heads + a + 1])
                    ins.then_inc(done["E"], 1)
                elif kind == "VA":
                    keep_turned(act, key, lambda o, i: nc.scalar.activation(o, i, ACT.Copy)).then_inc(done["VA"], 1)
                elif kind == "XA":
                    b, = key
                    wait(act, "UD", "xT", "X0", b, 1)
                    attentions_over(act)
                    if b:
                        wait(act, "UP", "f0", 0, FFN // 128 - 1)
                    nc.scalar.activation(xTH[:, :, :], xT[:, :, T * b:T * b + T], ACT.Copy).then_inc(done["XA"], 1)
                elif kind == "ZA":
                    b, _ = key
                    wait(act, "ZD", b, 0)
                    link(nc.scalar.activation(m_z[:, b, 2], m_z[:, b, 1], ACT.Exp))
                    link(nc.scalar.activation(m_z[:, b, 3], m_z[:, b, 2], ACT.Identity, bias=1.0))
                    nc.scalar.activation(m_z[:, b, 4], m_z[:, b, 3], ACT.Ln).then_inc(done["ZA"], 1)
                elif kind == "UA":
                    u = key
                    wait(act, "UP", *u)
                    if u[0] == "cT":
                        _, sg, c = u
                        dst = (ctxT0, ctxT1)[c]
                        n = (128, CC - 128)[c]
                        ins = nc.scalar.activation(dst[0:n, 512 * sg:512 * sg + 512], p_unit[0:n, :], ACT.Copy,
                                                   accum_out=(ctx_sum0, ctx_sum1)[c][:, sg:sg + 1])
                    elif u[0] == "rb":
                        G = group_no[u[1:]]
                        if G:
                            wait(act, "ON", *groups[G - 1])
                        ins = nc.scalar.activation(spread[:, :], p_unit[:, :], ACT.Copy)
                    elif u[0] in ("q", "k"):
                        place_free(act, u)
                        dst = by_layer(u[1], splitH_a, splitH_b)[:, place_of[u], :]
                        if u[1] == "X0":
                            act.wait_ge(x0_scaled, 1)
                            bias = (x0_bq if u[0] == "q" else x0_bk)[:, u[3]:u[3] + 1]
                            ins = nc.scalar.activation(dst, p_unit[:, :], ACT.Identity, bias=bias)
                        else:
                            ins = nc.scalar.activation(dst, p_unit[:, :], ACT.Copy)
                    elif u[0] == "v":
                        _, L, b, j = u
                        if L == "X1":
                            P2 = 4 * b + j // 2
                            if P2 >= 2:
                                wait(act, "AV", "X1", (P2 - 2) // 4, (P2 - 2) % 4, TT - 1, 1)
                            dst = x1_v[:, P2 % 2, 4 * (j % 2):4 * (j % 2) + 4, :]
                        elif L == "A1":
                            dst = a1_v[:, b, 2 * j:2 * j + 2, :]
                        else:
                            dst = a0_v[:, b, 2 * j:2 * j + 2, 0:256]
                        ins = nc.scalar.activation(dst, p_unit[:, :].rearrange("p (j n) -> p j n", n=dst.shape[-1]),
                                                   ACT.Copy)
                    elif u[0] in ("f0", "f1"):
                        j = int(u[0] == "f1")
                        act.wait_ge(f_scaled, 2)
                        m = relu_no[u]
                        if m >= 2:
                            wait(act, "FS", *relu_key(relu_units[m - 2]))
                        ins = nc.scalar.activation(relu[:, m % 2, :], bank(u), ACT.Relu, scale=f_scale[:, j:j + 1])
                    elif u[0] == "mh":
                        _, b, e = u
                        ins = nc.scalar.activation(m_h[:, b, e, :], bank(u), ACT.Silu, bias=m_b1[:, e:e + 1])
                    elif u[0] == "mc":
                        ins = nc.scalar.activation(m_gateT[:, u[1], :], bank(u)[0:NE + 1, :], ACT.Copy)
                    ins.then_inc(done["UA"], 1)

        @block.vector
        def _(dve):
            links = [0]

            def link(ins):
                links[0] += 1
                ins.then_inc(dve_chain, 1)
                dve.wait_ge(dve_chain, links[0])

            def statistics(b, hf):
                for i in (2 * hf, 2 * hf + 1):
                    ins = nc.vector.bn_stats(stats[:, tokens(b, i), :], x[:, tokens(b, i), :])
                return ins

            dve.wait_ge(a0_loaded, 64)
            for j in range(2):
                for c in range(2):
                    raw = a0_raw[:, j, c, :].rearrange("p (h d) -> p h d", d=3)
                    w = a0_wqk[:, c, 64 * j:64 * j + 64].rearrange("p (h d) -> p h d", d=4)
                    link(nc.vector.tensor_tensor(a0_tmp[:, :], a0_raw[:, j, c, :], a0_dirs[:, :], ALU.mult))
                    nc.vector.tensor_reduce(w[:, :, 3], a0_tmp[:, :].rearrange("p (h d) -> p h d", d=3), AX.X, ALU.add)
                    if j == 0:
                        link(nc.vector.tensor_scalar(w[:, :, 0:3], raw, a0_scale[:, 0:1], None, ALU.mult))
                    else:
                        link(nc.vector.tensor_copy(w[:, :, 0:3], raw))
            nc.vector.tensor_copy(a0_tmp[:, :], a0_raw[:, 0, 0, :]).then_inc(wqk_ready, 1)

            for kind, key in sched.steps:
                if kind == "QD":
                    stack_whole(dve, "A0", key[0], 0)
                    dve.wait_ge(heads_marked, 1)
                    mask_queries(nc.vector, *key).then_inc(done["QD"], 1)
                elif kind == "M":
                    L = key[0]
                    n = tile_no[key]
                    _, heads, w = tile_facts(key)
                    w_all = w if heads == 2 else LAYERS[L]["NK"]
                    wait(dve, "S", *key)
                    src = p_scores[:, n % 2, :].rearrange("p (a s) -> p a s", a=heads)[:, :, 0:w_all]
                    m = nmax[:, n % 4, 0:heads]
                    ins = nc.vector.tensor_reduce(m, src, AX.X, ALU.max, negate=True)
                    if L == "X0":
                        link(ins)
                        ins = nc.vector.tensor_scalar(m, m, CLAMP, -CLAMP, ALU.min, ALU.max)
                    ins.then_inc(done["M"], 1)
                elif kind == "CL":
                    n = tile_no[key]
                    wait(dve, "E", *key)
                    pr = prob_a[:, n % NP_SLOTS, :]
                    nc.vector.tensor_scalar(pr, pr, x0_lo[:, n % 4:n % 4 + 1], 1.0, ALU.max, ALU.min)\
                      .then_inc(done["CL"], 1)
                elif kind == "DN":
                    wait(dve, "AV", *key, TT - 1, parts(key[0]) - 1)
                    wait(dve, "UP", "wo", "A0", 1, 1)
                    nc.vector.tensor_copy(x0_raw, p_out[:, :]).then_inc(done["DN"], 1)
                elif kind == "NF":
                    wait(dve, "E", *phases[0][-1])
                    each = x0_sums[:, :, :, :, :].rearrange("p b g i a -> p (b g i a)")
                    link(nc.vector.tensor_tensor(x0_nans, each, each, ALU.not_equal))
                    nc.vector.tensor_reduce(x0_nan[:, 0:1], x0_nans, AX.X, ALU.add).then_inc(done["NF"], 1)
                elif kind == "GN":
                    b, = key
                    wait(dve, "UD", "nf")
                    wait(dve, "UD", "mv")
                    wait(dve, "ON", "X0", b, 3)
                    nc.vector.copy_predicated(
                        outT_x[:, b], x0_nan[:, 1:2].bitcast(I32).unsqueeze(2).to_broadcast([128, 4, T]),
                        x0_mean[:, b, :].unsqueeze(2).to_broadcast([128, 4, T])).then_inc(done["GN"], 1)
                elif kind == "VD":
                    keep_turned(dve, key, lambda o, i: nc.vector.tensor_copy(o, i)).then_inc(done["VD"], 1)
                elif kind == "RC":
                    G = group_no[key]
                    last = tuple([*key, TT - 1, LAYERS[key[0]]["G"] // LAYERS[key[0]]["HT"] - 1])
                    wait(dve, "E", *last)
                    ng = LAYERS[key[0]]["G"]
                    link(nc.vector.reciprocal(rsum[:, G % 2, :, 0:ng], sums[:, G % 2, :, 0:ng]))
                    if G:
                        wait(dve, "UP", "rb", *groups[G - 1])
                    nc.vector.tensor_copy(rwide[:, :, :].rearrange("p i (a r) -> p i a r", a=ng),
                                          rsum[:, G % 2, :, 0:ng].unsqueeze(3).to_broadcast([128, TT, ng, 128 // ng]))\
                      .then_inc(done["RC"], 1)
                elif kind == "ON":
                    L, b, g = key
                    G = group_no[key]
                    wait(dve, "UA", "rb", *key)
                    if L == "X0":
                        wait(dve, "DN", *key)
                        nc.vector.tensor_tensor(outT_x[:, b, g, :], x0_raw, spread[:, :], ALU.mult)\
                          .then_inc(done["ON"], 1)
                        continue
                    wait(dve, "AV", *key, TT - 1, parts(key[0]) - 1)
                    if g == 0 and prev_batch[(L, b)] and prev_batch[(L, b)][0] != "X0":
                        wait(dve, "UP", "wo", *prev_batch[(L, b)], 1)
                    nc.vector.tensor_tensor(by_layer(L, outT_a, outT_b)[:, g, :], p_out[:, :], spread[:, :], ALU.mult)\
                      .then_inc(done["ON"], 1)
                elif kind == "LS":
                    L, b = key
                    wait(dve, "UD", *{"F": ("f2", b, 1), "M": ("my", b, 1)}.get(L, ("wo", L, b, 1)))
                    for i in range(TT):
                        ins = nc.vector.bn_aggr(mv[:, tokens(b, i), :], stats[:, tokens(b, i), :])
                    ins.then_inc(done["LS"], 1)
                elif kind == "XD":
                    b, = key
                    wait(dve, "XA", b)
                    if b:
                        wait(dve, "UP", "f0", 0, FFN // 128 - 1)
                    nc.vector.tensor_tensor(xTL[:, :, :], xT[:, :, T * b:T * b + T], xTH[:, :, :].bitcast(F32),
                                            ALU.subtract).then_inc(done["XD"], 1)
                elif kind == "FW":
                    j, = key
                    attentions_over(dve)
                    if j > FFN // 128:
                        wait(dve, "UP", "wo", "X0", 1, 1)
                    dve.wait_ge(signs_loaded, 48)
                    if j == 0:
                        ins = nc.vector.tensor_tensor(k0[:, :, :], k0_words[:, 0:2, :].bitcast(U8), k0_words[:, 2:4, :].bitcast(U8), ALU.subtract)
                    elif j <= FFN // 128:
                        ins = nc.vector.tensor_scalar(k1[:, j - 1, :], k1_words[:, j - 1, :].bitcast(U8), 2.0, -1.0, ALU.mult, ALU.add)
                    else:
                        ins = nc.vector.tensor_scalar(k2[:, :, :], k2_words[:, :, :].bitcast(U8), 2.0, -1.0, ALU.mult, ALU.add)
                    ins.then_inc(done["FW"], 1)
                elif kind == "FS":
                    j, b, o = key
                    u = (f"f{j}", b, o)
                    wait(dve, "UA", *u)
                    if j:
                        wait(dve, "UP", "wo", "X0", 1, 1)
                    if b:
                        wait(dve, "UP", *(("f1", 0, FFN // 128 - 1) if j == 0 else ("f2", 0, 1)))
                    r = relu[:, relu_no[u] % 2, :]
                    link(nc.vector.tensor_copy(hH[j][:, o, :], r))
                    nc.vector.tensor_tensor(hL[j][:, o, :], r, hH[j][:, o, :].bitcast(F32), ALU.subtract)\
                      .then_inc(done["FS"], 1)
                elif kind == "ZD":
                    b, stage = key
                    z = [m_z[:, b, j] for j in range(8)]
                    if stage == 0:
                        wait(dve, "UD", "mr", b)
                        nc.vector.scalar_tensor_tensor(out=z[1], in0=z[0], scalar=-1.0, in1=z[0], op0=ALU.mult,
                                                       op1=ALU.min).then_inc(done["ZD"], 1)
                    elif stage == 1:
                        wait(dve, "ZA", b, 0)
                        link(nc.vector.tensor_scalar(z[5], z[3], 1.0, None, ALU.is_equal))
                        nc.vector.tensor_tensor(z[4], z[4], z[5], ALU.add)
                        link(nc.vector.scalar_tensor_tensor(out=z[6], in0=z[3], scalar=-1.0, in1=z[5], op0=ALU.add,
                                                            op1=ALU.add))
                        nc.vector.tensor_tensor(z[4], z[4], z[2], ALU.mult)
                        link(nc.vector.reciprocal(z[6], z[6]))
                        link(nc.vector.tensor_tensor(z[4], z[4], z[6], ALU.mult))
                        nc.vector.scalar_tensor_tensor(out=z[7], in0=z[0], scalar=0.0, in1=z[4], op0=ALU.max,
                                                       op1=ALU.add).then_inc(done["ZD"], 1)
                    else:
                        wait(dve, "ZP", b)
                        dve.wait_ge(m_consts, 1)
                        mine = z[1].unsqueeze(3).to_broadcast([128, TT, NE, NE])
                        other = z[1].unsqueeze(2).to_broadcast([128, TT, NE, NE])
                        nc.vector.tensor_tensor(m_cmp[:, 0], other, mine, ALU.is_gt)
                        link(nc.vector.tensor_tensor(m_cmp[:, 1], other, mine, ALU.is_equal))
                        link(nc.vector.tensor_tensor(m_cmp[:, 1], m_cmp[:, 1],
                                                     m_lt[:, :, :].unsqueeze(1).to_broadcast([128, TT, NE, NE]), ALU.mult))
                        link(nc.vector.tensor_tensor(m_cmp[:, 2], m_cmp[:, 0], m_cmp[:, 1], ALU.add))
                        link(nc.vector.tensor_reduce(z[2], m_cmp[:, 2], AX.X, ALU.add))
                        nc.vector.scalar_tensor_tensor(out=m_gate[:, b, :, 0:NE], in0=z[2], scalar=2.0, in1=z[1],
                                                       op0=ALU.is_lt, op1=ALU.mult).then_inc(done["ZD"], 1)
                elif kind == "LN":
                    L, b = key
                    wait(dve, "LP", L, b)
                    for i in range(TT):
                        t = tokens(b, i)
                        ins = nc.vector.tensor_scalar(x[:, t, :], x[:, t, :], mv[:, t, 0:1], rstd[:, t:t + 1],
                                                      ALU.subtract, ALU.mult)
                    ins.then_inc(done["LN"], 1)
                elif kind == "UD":
                    u = key
                    wait(dve, "UP", *u)
                    if u[0] == "dt":
                        if group_no[u[1:]]:
                            wait(dve, "UP", "rb", *groups[group_no[u[1:]] - 1])
                        link(nc.vector.reciprocal(rsum[:, 0], p_unit[:, :].rearrange("p (i a r) -> p i a r", i=TT, a=4)[:, :, :, 16]))
                        ins = nc.vector.tensor_copy(rwide[:, :, :].rearrange("p i (a r) -> p i a r", a=4),
                                                    rsum[:, 0].unsqueeze(3).to_broadcast([128, TT, 4, 32]))
                    elif u[0] == "mv":
                        sums_of = p_unit[:, 0:16].rearrange("p (g b s) -> p b g s", g=4, b=B)
                        link(nc.vector.tensor_reduce(x0_mean[:, :, :], sums_of, AX.X, ALU.add))
                        ins = nc.vector.scalar_tensor_tensor(
                            out=x0_mean[:, :, :], in0=x0_mean[:, :, :], scalar=1.0 / NKV,
                            in1=x0_bvT[:, :].unsqueeze(1).to_broadcast([128, B, 4]), op0=ALU.mult, op1=ALU.add)
                    elif u[0] == "nf":
                        ins = nc.vector.tensor_scalar(x0_nan[:, 1:2], p_unit[:, 0:1], 0.0, None, ALU.is_gt)
                    elif u[0] == "xT":
                        _, L, b, c = u
                        ins = nc.vector.tensor_copy(xT[:, c, T * b:T * b + T], p_unit[:, :])
                    elif u[0] in ("q", "k"):
                        wait(dve, "UA", *u)
                        place_free(dve, u)
                        pl = place_of[u]
                        if u[1] == "X0":
                            bias = (x0_bq if u[0] == "q" else x0_bk)[:, u[3]:u[3] + 1]
                            ins = nc.vector.scalar_tensor_tensor(
                                out=splitL_a[:, pl, :], in0=p_unit[:, :], scalar=bias,
                                in1=splitH_a[:, pl, :].bitcast(F32), op0=ALU.add, op1=ALU.subtract)
                        else:
                            splitH, splitL = by_layer(u[1], splitH_a, splitH_b), by_layer(u[1], splitL_a, splitL_b)
                            ins = nc.vector.tensor_tensor(splitL[:, pl, :], p_unit[:, :],
                                                          splitH[:, pl, :].bitcast(F32), ALU.subtract)
                    elif u[0] == "v":
                        _, L, b, j = u
                        ins = nc.vector.tensor_tensor(
                            x0_v[:, b, 2 * j:2 * j + 2, 0:272].rearrange("p j (h c) -> p j h c", c=17)[:, :, :, 0:16],
                            p_unit[:, :].rearrange("p (j h c) -> p j h c", j=2, c=16),
                            x0_bv[:, :].rearrange("p (h c) -> p h c", c=16).unsqueeze(1).to_broadcast([128, 2, 16, 16]),
                            ALU.add)
                    elif u[0] == "wo":
                        _, L, b, hf = u
                        if L == "X0":
                            wait(dve, "BA", L, b)
                        xs = x[:, tokens(b, 2 * hf):tokens(b, 2 * hf) + 2, :]
                        new = p_unit[:, :].rearrange("p (i c) -> p i c", i=2)
                        if L == "A1":
                            link(nc.vector.scalar_tensor_tensor(out=xs, in0=xs, scalar=2.0, in1=new,
                                                                op0=ALU.mult, op1=ALU.add))
                        else:
                            link(nc.vector.tensor_tensor(xs, new, xs, ALU.add))
                        ins = statistics(b, hf)
                    elif u[0] in ("f2", "my"):
                        _, b, hf = u
                        xs = x[:, tokens(b, 2 * hf):tokens(b, 2 * hf) + 2, :]
                        new = bank(u).rearrange("p (i c) -> p i c", i=2)
                        if u[0] == "f2":
                            dve.wait_ge(f_scales_loaded, 48)
                            link(nc.vector.scalar_tensor_tensor(out=xs, in0=new, scalar=f_scale[:, 2:3], in1=xs,
                                                                op0=ALU.mult, op1=ALU.add))
                        else:
                            link(nc.vector.tensor_tensor(xs, new, xs, ALU.add))
                        ins = statistics(b, hf)
                    elif u[0] == "mr":
                        _, b = u
                        ins = nc.vector.tensor_tensor(
                            m_z[:, b, 0], bank(u)[:, 0:TT * NE].rearrange("p (i e) -> p i e", e=NE),
                            m_br[:, :].unsqueeze(1).to_broadcast([128, TT, NE]), ALU.add)
                    elif u[0] == "mb":
                        _, b, e = u
                        wait(dve, "UA", "mh", b, e)
                        ins = nc.vector.tensor_tensor(m_h[:, b, e, :], m_h[:, b, e, :], bank(u), ALU.mult)
                    ins.then_inc(done["UD"], 1)

        @block.tensor
        def _(pe):
            pe.wait_ge(consts_ready, 2)

            def product(o, pairs):
                for n, (a, m) in enumerate(pairs):
                    ins = nc.tensor.matmul(o, a, m, start=(n == 0), stop=(n == len(pairs) - 1))
                return ins

            for kind, key in sched.steps:
                if kind == "S":
                    L, b, g, i, k = key
                    n = tile_no[key]
                    h0, heads, w = tile_facts(key)
                    back = tile_back(key, 2)
                    if back:
                        wait(pe, "E", *back)
                    if L == "A0":
                        stack_whole(pe, L, b, 0)
                        wait(pe, "QD" if 4 * b + g < 2 else "QM", b, g)
                        for a in range(2):
                            h = h0 + a
                            o = p_scores[:, n % 2, 512 * a:512 * a + w]
                            q = a0_qm[:, 4 * (g % 2) + h % 4, 128 * i:128 * i + 128]
                            nc.tensor.matmul(o, q, a0_ks[:, b, h // 8, 0:w], start=True, stop=False)
                            ins = nc.tensor.matmul(o[:, w - 128:w], identb[:, :], hidden[:, :], start=False, stop=True)
                    elif L == "X0":
                        p = h0 // 2
                        stack_whole(pe, L, b, p)
                        P = b * 8 + p
                        for s in range(2):
                            ins = nc.tensor.matmul(p_scores[:, n % 2, 512 * s:512 * s + 512],
                                                   x0_qs[:, P % 4, h0 % 2, 128 * i:128 * i + 128],
                                                   x0_ks[:, P % 4, 512 * s:512 * s + 512], start=True, stop=True)
                    else:
                        if key == phases[1][0]:
                            wait(pe, "UD", "f2", 1, 1)
                        p = h0 // 2
                        stack_whole(pe, L, b, p)
                        st = stacks[:, pair_no(L, b, p) % 2]
                        for a in range(2):
                            q_at = 512 * (a if L == "A1" else h0 % 2) + 128 * i
                            for part in range(2):
                                k_at = 1024 + (512 * part if L == "A1" else (2 * (h0 % 2) + part) * 1024 + 512 * a)
                                ins = nc.tensor.matmul(p_scores[:, n % 2, 512 * a:512 * a + 512],
                                                       st[:, q_at:q_at + 128], st[:, k_at:k_at + 512],
                                                       start=(part == 0), stop=(part == 1))
                    ins.then_inc(done["S"], 1)
                elif kind == "T":
                    *t, half = key
                    t = tuple(t)
                    n = tile_no[t]
                    wait(pe, "CL" if t[0] == "X0" else "E", *t)
                    turned_bank_free(pe, t, half)
                    for j, bl in enumerate(blocks_of(t, half)):
                        ins = nc.tensor.transpose(p_turn[:, half, 128 * j:128 * j + 128],
                                                  by_layer(t[0], prob_a, prob_b)[:, n % NP_SLOTS, 128 * bl:128 * bl + 128], ident[:, :])
                    ins.then_inc(done["T"], 1)
                elif kind == "AV":
                    L, b, g, i, part = key
                    p = LAYERS[L]
                    G = group_no[(L, b, g)]
                    for k in range(p["G"] // p["HT"]):
                        t = (L, b, g, i, k)
                        for half in ((part,) if parts(L) == 2 else range(2)):
                            wait(pe, turned_by(L, tile_no[t], half), *t, half)
                    if i == 0 and part == 0 and G:
                        wait(pe, "DN" if groups[G - 1][0] == "X0" else "ON", *groups[G - 1])
                    if i == 0:
                        values_ready(pe, L, b, g)
                    chunks = i + 1 if L == "A0" else p["NK"] // 128
                    places, probT = by_layer(L, PT_A, PT_B), by_layer(L, probT_a, probT_b)
                    for j in range(4 * part, 4 * part + 4) if parts(L) == 2 else range(chunks):
                        for a in range(p["G"]):
                            h = p["G"] * g + a
                            k, in_tile = a // p["HT"], a % p["HT"]
                            n = tile_no[(L, b, g, i, k)]
                            rows = 128 // p["G"]
                            ins = nc.tensor.matmul(
                                p_out[rows * a:rows * a + rows, 128 * i:128 * i + 128],
                                values(L, b, h, j), probT[:, n % places, 4 * in_tile + j if p["HT"] == 2 else j, :],
                                start=(j == 0), stop=(j == chunks - 1))
                    ins.then_inc(done["AV"], 1)
                elif kind == "UP":
                    u = key
                    bank_free(pe, u)
                    if u in (("f0", 0, 0), ("mr", 0)):
                        wait(pe, "E", *phases[0 if u[0] == "f0" else 1][-1])
                    if u[0] == "xT":
                        _, L, b, c = u
                        if L == "in":
                            pe.wait_ge(x_loaded, 32)
                        else:
                            wait(pe, "LN", L, b)
                        for i in range(TT):
                            ins = nc.tensor.transpose(p_unit[:, 128 * i:128 * i + 128],
                                                      x[:, tokens(b, i), 128 * c:128 * c + 128], ident[:, :])
                    elif u[0] == "cT":
                        _, sg, c = u
                        pe.wait_ge(ctx_loaded, 16)
                        n = (128, CC - 128)[c]
                        for i in range(4):
                            ins = nc.tensor.transpose(p_unit[0:n, 128 * i:128 * i + 128],
                                                      ctx_raw[:, 4 * sg + i, 128 * c:128 * c + n], ident[:, :])
                    elif u[0] == "dt":
                        wait(pe, "DN", *u[1:])
                        for i in range(TT):
                            ins = nc.tensor.transpose(p_unit[:, 128 * i:128 * i + 128], x0_raw[:, 128 * i:128 * i + 128],
                                                      ident[:, :])
                    elif u[0] == "mv":
                        pe.wait_ge(x0_loaded, 16 * 13)
                        keys_turned(pe, 3)
                        for h in range(16):
                            a = 32 * (h % 4)
                            ins = product(p_unit[a:a + 32, 4 * (h // 4):4 * (h // 4) + 4],
                                          [(x0_wv0[:, 16 * h:16 * h + 32], ctx_sum0[:, :]),
                                           (x0_wv1[:, 16 * h:16 * h + 32], ctx_sum1[:, :])])
                    elif u[0] == "nf":
                        wait(pe, "NF")
                        ins = product(p_unit[:, 0:1], [(ones[:, :], x0_nan[:, 0:1])])
                    elif u[0] == "rb":
                        if u[1] == "X0":
                            wait(pe, "UD", "dt", *u[1:])
                        else:
                            wait(pe, "RC", *u[1:])
                        for i in range(TT):
                            ins = nc.tensor.transpose(p_unit[:, 128 * i:128 * i + 128], rwide[:, i, :], ident[:, :])
                    elif u[0] in ("q", "k"):
                        L, b = u[1], u[2]
                        if L == "A0":
                            pe.wait_ge(wqk_ready, 1)
                            wait(pe, "UD", "xT", "in", b, 1)
                            ins = product(p_unit[:, :], [(a0_wqk[:, c, :], xT[:, c, T * b:T * b + T]) for c in range(2)])
                        elif L == "A1":
                            pe.wait_ge(a1_scaled, 1)
                            wait(pe, "UD", "xT", "F", b, 1)
                            w, m = (a1_wq if u[0] == "q" else a1_wk), u[3]
                            ins = product(p_unit[:, :], [(w[:, c, 128 * m:128 * m + 128], xT[:, c, T * b:T * b + T])
                                                         for c in range(2)])
                        elif L == "X1" and u[0] == "q":
                            pe.wait_ge(x1_scaled, 1)
                            wait(pe, "UD", "xT", "A1", b, 1)
                            m = u[3]
                            ins = product(p_unit[:, :], [(x1_wq[:, c, 128 * m:128 * m + 128], xT[:, c, T * b:T * b + T])
                                                         for c in range(2)])
                        elif L == "X1":
                            pe.wait_ge(x1_loaded, 16 * 7)
                            m, s = u[3], u[4]
                            at = NKV * b + 512 * s
                            ins = product(p_unit[:, :], [(x1_wk0[:, 128 * m:128 * m + 128], ctxT0[:, at:at + 512]),
                                                         (x1_wk1[:, 128 * m:128 * m + 128], ctxT1[:, at:at + 512])])
                        elif u[0] == "q":
                            pe.wait_ge(x0_scaled, 1)
                            wait(pe, "UD", "xT", "A0", b, 1)
                            m = u[3]
                            ins = product(p_unit[:, :], [(x0_wq[:, c, 128 * m:128 * m + 128], xT[:, c, T * b:T * b + T])
                                                         for c in range(2)])
                        else:
                            m, s = u[3], u[4]
                            keys_turned(pe, 2 * b + s)
                            pe.wait_ge(x0_loaded, 16 * 13)
                            at = NKV * b + 512 * s
                            ins = product(p_unit[:, :], [(x0_wk0[:, 128 * m:128 * m + 128], ctxT0[:, at:at + 512]),
                                                         (x0_wk1[:, 128 * m:128 * m + 128], ctxT1[:, at:at + 512])])
                    elif u[0] == "v" and u[1] == "X1":
                        _, L, b, j = u
                        pe.wait_ge(x1_loaded, 16 * 7)
                        m = 128 * (j // 2)
                        for r in range(4):
                            at = NKV * b + 128 * (4 * (j % 2) + r)
                            ins = product(p_unit[:, 128 * r:128 * r + 128],
                                          [(ctxT0[:, at:at + 128], x1_wv0[:, m:m + 128]),
                                           (ctxT1[:, at:at + 128], x1_wv1[:, m:m + 128])])
                    elif u[0] == "v":
                        _, L, b, j = u
                        for r in range(2):
                            i = 2 * j + r
                            o = p_unit[:, 256 * r:256 * r + 256]
                            if L == "A1":
                                pe.wait_ge(a1_loaded, 64)
                                wait(pe, "UD", "xT", "F", b, 1)
                                at = T * b + 128 * i
                                ins = product(o, [(xT[:, c, at:at + 128], a1_wv[:, c, :]) for c in range(2)])
                            elif L == "A0":
                                pe.wait_ge(a0w_loaded, 16 * 5)
                                wait(pe, "UD", "xT", "in", b, 1)
                                at = T * b + 128 * i
                                ins = product(o, [(xT[:, c, at:at + 128], a0_wv[:, c, :]) for c in range(2)])
                            else:
                                keys_turned(pe, 2 * b + i // 4)
                                pe.wait_ge(x0_loaded, 16 * 13)
                                at = NKV * b + 128 * i
                                ins = product(o, [(ctxT0[:, at:at + 128], x0_wv0[:, 0:C]), (ctxT1[:, at:at + 128], x0_wv1[:, 0:C])])
                    elif u[0] == "wo":
                        _, L, b, hf = u
                        wo = {"A0": wo_rows, "X0": wo_rows, "A1": a1_wo, "X1": x1_wo}[L]
                        outT = outT_x[:, b] if L == "X0" else by_layer(L, outT_a, outT_b)
                        if L == "X0":
                            pe.wait_ge(x0_wo_loaded, 64)
                            wait(pe, "GN", b)
                        wait(pe, "ON", L, b, LAYERS[L]["H"] // LAYERS[L]["G"] - 1)
                        for r in range(2):
                            i = 2 * hf + r
                            ins = product(p_unit[:, 256 * r:256 * r + 256],
                                          [(outT[:, g, 128 * i:128 * i + 128], wo[:, g, :])
                                           for g in range(LAYERS[L]["H"] // LAYERS[L]["G"])])
                    elif u[0] == "f0":
                        _, b, o = u
                        wait(pe, "XA", b)
                        wait(pe, "XD", b)
                        wait(pe, "FW", 0)
                        ins = product(bank(u), [(k0[:, c, 128 * o:128 * o + 128], part[:, c, :])
                                                for c in range(2) for part in (xTH, xTL)])
                    elif u[0] == "f1":
                        _, b, o = u
                        wait(pe, "FS", 0, b, FFN // 128 - 1)
                        wait(pe, "FW", FFN // 128)
                        ins = product(bank(u), [(k1[:, c, 128 * o:128 * o + 128], part[:, c, :])
                                                for c in range(FFN // 128) for part in (hH[0], hL[0])])
                    elif u[0] == "f2":
                        _, b, hf = u
                        wait(pe, "FS", 1, b, FFN // 128 - 1)
                        wait(pe, "FW", FFN // 128 + 1)
                        for r in range(2):
                            at = 128 * (2 * hf + r)
                            ins = product(bank(u)[:, 256 * r:256 * r + 256],
                                          [(part[:, c, at:at + 128], k2[:, c, :])
                                           for c in range(FFN // 128) for part in (hH[1], hL[1])])
                    elif u[0] == "mr":
                        _, b = u
                        pe.wait_ge(m_loaded, 16 * 18)
                        wait(pe, "UD", "xT", "X1", b, 1)
                        for i in range(TT):
                            at = T * b + 128 * i
                            ins = product(bank(u)[:, NE * i:NE * i + NE],
                                          [(xT[:, c, at:at + 128], m_wr[:, c, :]) for c in range(2)])
                    elif u[0] == "mh":
                        _, b, e = u
                        ins = product(bank(u), [(m_w1[:, e, c, :], xT[:, c, T * b:T * b + T]) for c in range(2)])
                    elif u[0] == "mc":
                        _, b = u
                        wait(pe, "ZD", b, 2)
                        for i in range(TT):
                            ins = nc.tensor.transpose(bank(u)[0:NE + 1, 128 * i:128 * i + 128], m_gate[:, b, i, :],
                                                      ident[:, :])
                    elif u[0] == "mb":
                        _, b, e = u
                        for i in range(TT):
                            ins = nc.tensor.transpose(bank(u)[:, 128 * i:128 * i + 128],
                                                      m_gate[:, b, i, e:e + 1].to_broadcast([128, 128]), ident[:, :])
                    elif u[0] == "my":
                        _, b, hf = u
                        wait(pe, "UD", "mb", b, NE - 1)
                        wait(pe, "UA", "mc", b)
                        for r in range(2):
                            at = 128 * (2 * hf + r)
                            ins = product(bank(u)[:, 256 * r:256 * r + 256],
                                          [(m_h[:, b, e, at:at + 128], m_w2[:, e, :]) for e in range(NE + 1)]
                                          + [(m_gateT[:, b, at:at + 128], m_b2[:, :])])
                    ins.then_inc(done["UP"], 1)



def kernel(**inputs):
    import concourse.bacc as bacc
    from concourse.bass_utils import run_bass_kernel_spmd

    nc = bacc.Bacc("TRN2", target_bir_lowering=False, num_devices=1)
    arrays, d = {}, {}
    for name, value in inputs.items():
        a = np.ascontiguousarray(value)
        if a.dtype == np.bool_:
            a = a.view(np.int32)
        arrays[f"in_{name}"] = a
        d[name] = nc.dram_tensor(f"in_{name}", a.shape, mybir.dt.from_np(a.dtype), kind="ExternalInput").ap()
    out = nc.dram_tensor("out_x", (B, T, C), F32, kind="ExternalOutput").ap()
    decoder(nc, d, out)
    r = run_bass_kernel_spmd(nc, [arrays], core_ids=[0])
    return r.results[0]["out_x"]
```
